# Optimizing a Trainium2 kernel written in Bass

```python
import numpy as np
import jax
import jax.numpy as jnp

def _softmax(x, axis=-1):
    return jax.nn.softmax(x, axis=axis)

def _gelu(x):
    return jax.nn.gelu(x, approximate=True)

def _silu(x):
    return jax.nn.silu(x)

def _sigmoid(x):
    return jax.nn.sigmoid(x)

def _layernorm(x, axis=-1, eps=1e-05):
    m = jnp.mean(x, axis=axis, keepdims=True)
    v = jnp.var(x, axis=axis, keepdims=True)
    return (x - m) / jnp.sqrt(v + eps)

def _scatter_add(tgt, idx, src, axis=0):
    return tgt.at[idx].add(src)

def _segment_sum(src, seg, n):
    return jax.ops.segment_sum(src, seg, n)
kernel_name = 'mk_decoder_postln_d1_seqx_r8_509149'

def setup_inputs(seed: int=0):
    np.random.seed(seed)
    _w = jnp.asarray

    def _rec_inputs():
        import jax
        import jax.numpy as jnp
        _rk = jax.random.key(seed)
        x = -0.0003929 + 0.9999 * jax.random.normal(jax.random.fold_in(_rk, 1), (4, 256, 256), jnp.float32)
        _lenS = 256 - jax.random.randint(jax.random.fold_in(_rk, 7), (4,), 0, max(1, 256 // 4) + 1, jnp.int32)
        _lenS2 = 256 - jax.random.randint(jax.random.fold_in(_rk, 8), (4,), 0, max(1, 256 // 4) + 1, jnp.int32)
        _ctx_2048P = jax.random.normal(jax.random.fold_in(_rk, 11), (4, 16, 256), jnp.float32)
        _ctx_2048c = jax.random.dirichlet(jax.random.fold_in(_rk, 511), 0.3 * jnp.ones((16,), jnp.float32), (4, 256))
        _ctx_2048t = jnp.einsum('bsk,bkd->bsd', _ctx_2048c, _ctx_2048P)
        _ctx_2048t = _ctx_2048t * jax.lax.rsqrt(jnp.mean(jnp.square(_ctx_2048t)) + 1e-12) * 0.953939
        ctx_2048 = -0.000514642 + 1.00011 * (_ctx_2048t + 0.3 * jax.random.normal(jax.random.fold_in(_rk, 611), (4, 256, 256), jnp.float32))
        _validS = jnp.arange(256)[None, :] < _lenS[:, None]
        _validS2 = jnp.arange(256)[None, :] < _lenS2[:, None]
        _causal = jnp.tril(jnp.ones((256, 256), dtype=bool))
        mask_BxSxS2_ff0 = jnp.where(jnp.ones((4, 256, 256), dtype=bool), 0.0, -1000000000.0).astype(jnp.float32)
        return (x, ctx_2048, mask_BxSxS2_ff0)
    x, ctx_2048, mask_BxSxS2_ff0 = _rec_inputs()

    def _L0_attn_setup():
        import jax, jax.numpy as jnp
        import numpy as np
        HIDDEN = 256
        N_HEADS = 16
        N_KV_HEADS = 2
        HEAD_DIM = 128
        THETA = 10000.0
        SCALE = 0.08838834764831845
        SOFTCAP = 30.0

        def apply_rotary_emb(x, theta=THETA):
            B, S, H, D = x.shape
            inv_freq = 1.0 / theta ** (jnp.arange(0, D, 2, dtype=jnp.float32) / D)
            t = jnp.arange(S, dtype=jnp.float32)
            freqs = jnp.outer(t, inv_freq)
            cos = jnp.cos(freqs)[None, :, None, :]
            sin = jnp.sin(freqs)[None, :, None, :]
            x1, x2 = (x[..., :D // 2], x[..., D // 2:])
            out = jnp.concatenate([x1 * cos - x2 * sin, x1 * sin + x2 * cos], axis=-1)
            return out.astype(x.dtype)
        key = jax.random.key(seed)
        k1, k2, k3 = jax.random.split(key, 3)
        B, S = (2, 256)
        qkv_out = (N_HEADS + 2 * N_KV_HEADS) * HEAD_DIM
        hidden_states = jax.random.normal(k1, (B, S, HIDDEN), dtype=jnp.float32)
        Wqkv = jax.random.normal(k2, (HIDDEN, qkv_out), dtype=jnp.float32) * HIDDEN ** (-0.5)
        Wo = jax.random.normal(k3, (N_HEADS * HEAD_DIM, HIDDEN), dtype=jnp.float32) * (N_HEADS * HEAD_DIM) ** (-0.5)
        return {'hidden_states': hidden_states, 'Wqkv': Wqkv, 'Wo': Wo}
    _L0_attn_all = _L0_attn_setup()
    _L0_attn_in = {k: v for k, v in _L0_attn_all.items() if k in ('Wqkv', 'Wo')}
    del _L0_attn_all

    def _L0_xattn_setup():
        import jax, jax.numpy as jnp
        import numpy as np
        NUM_HEADS = 16
        EPS = 1e-08

        def _dyn_quant(x):
            s = jnp.maximum(jnp.max(jnp.abs(x), axis=-1, keepdims=True) / 127.0, EPS)
            q = jnp.clip(jnp.round(x / s), -127.0, 127.0)
            return (q, s)

        def _quant_weight(w):
            s = jnp.maximum(jnp.max(jnp.abs(w), axis=1, keepdims=True) / 127.0, EPS)
            q = jnp.clip(jnp.round(w / s), -127.0, 127.0)
            return (q, s)

        def _w8a8_linear(x, w, b):
            qx, sx = _dyn_quant(x)
            qw, sw = _quant_weight(w)
            y = jnp.einsum('bnc,oc->bno', qx, qw) * (sx * sw[:, 0])
            return y + b
        key = jax.random.key(seed)
        ks = jax.random.split(key, 9)
        B, N, L, C = (2, 512, 64, 256)
        sc = 0.02
        return {'x': jax.random.normal(ks[0], (B, N, C), jnp.float32), 'cond': jax.random.normal(ks[1], (B, L, C), jnp.float32), 'mask': jnp.zeros((B, N, L), jnp.float32), 'wq': jax.random.normal(ks[2], (C, C), jnp.float32) * sc, 'bq': jnp.zeros((C,), jnp.float32), 'wk': jax.random.normal(ks[3], (C, C), jnp.float32) * sc, 'bk': jnp.zeros((C,), jnp.float32), 'wv': jax.random.normal(ks[4], (C, C), jnp.float32) * sc, 'bv': jnp.zeros((C,), jnp.float32), 'wo': jax.random.normal(ks[5], (C, C), jnp.float32) * sc, 'bo': jnp.zeros((C,), jnp.float32)}
    _L0_xattn_all = _L0_xattn_setup()
    _L0_xattn_in = {k: v for k, v in _L0_xattn_all.items() if k in ('wq', 'bq', 'wk', 'bk', 'wv', 'bv', 'wo', 'bo')}
    del _L0_xattn_all

    def _L0_ffn_setup():
        import jax, jax.numpy as jnp
        import numpy as np
        N_BLOCKS = 16
        BLOCK_SIZE = 64
        TOP_K = N_BLOCKS // 4
        key = jax.random.key(seed)
        k1, k2, k3, k4, k5 = jax.random.split(key, 5)
        in_f, out_f = (256, 1024)
        x = jax.random.normal(k1, (2, 512, in_f), dtype=jnp.float32)
        Wr = jax.random.normal(k2, (N_BLOCKS, in_f), dtype=jnp.float32) * in_f ** (-0.5)
        br = jnp.zeros((N_BLOCKS,), dtype=jnp.float32)
        W1 = jax.random.normal(k3, (out_f, in_f), dtype=jnp.float32) * in_f ** (-0.5)
        W2 = jax.random.normal(k4, (in_f, out_f), dtype=jnp.float32) * out_f ** (-0.5)
        return {'x': x, 'Wr': Wr, 'br': br, 'W1': W1, 'W2': W2}
    _L0_ffn_all = _L0_ffn_setup()
    _L0_ffn_in = {k: v for k, v in _L0_ffn_all.items() if k in ('Wr', 'br', 'W1', 'W2')}
    del _L0_ffn_all
    return {'x': x, 'ctx_2048': ctx_2048, 'mask_BxSxS2_ff0': mask_BxSxS2_ff0, 'L0_attn_Wqkv': _L0_attn_in['Wqkv'], 'L0_attn_Wo': _L0_attn_in['Wo'], 'L0_xattn_wq': _L0_xattn_in['wq'], 'L0_xattn_bq': _L0_xattn_in['bq'], 'L0_xattn_wk': _L0_xattn_in['wk'], 'L0_xattn_bk': _L0_xattn_in['bk'], 'L0_xattn_wv': _L0_xattn_in['wv'], 'L0_xattn_bv': _L0_xattn_in['bv'], 'L0_xattn_wo': _L0_xattn_in['wo'], 'L0_xattn_bo': _L0_xattn_in['bo'], 'L0_ffn_Wr': _L0_ffn_in['Wr'], 'L0_ffn_br': _L0_ffn_in['br'], 'L0_ffn_W1': _L0_ffn_in['W1'], 'L0_ffn_W2': _L0_ffn_in['W2']}

def reference(x, ctx_2048, mask_BxSxS2_ff0, L0_attn_Wqkv, L0_attn_Wo, L0_xattn_wq, L0_xattn_bq, L0_xattn_wk, L0_xattn_bk, L0_xattn_wv, L0_xattn_bv, L0_xattn_wo, L0_xattn_bo, L0_ffn_Wr, L0_ffn_br, L0_ffn_W1, L0_ffn_W2):
    import jax
    import jax.numpy as jnp

    def _L0_attn_ref(hidden_states, Wqkv, Wo):
        import jax, jax.numpy as jnp
        import numpy as np
        HIDDEN = 256
        N_HEADS = 16
        N_KV_HEADS = 2
        HEAD_DIM = 128
        THETA = 10000.0
        SCALE = 0.08838834764831845
        SOFTCAP = 30.0

        def apply_rotary_emb(x, theta=THETA):
            B, S, H, D = x.shape
            inv_freq = 1.0 / theta ** (jnp.arange(0, D, 2, dtype=jnp.float32) / D)
            t = jnp.arange(S, dtype=jnp.float32)
            freqs = jnp.outer(t, inv_freq)
            cos = jnp.cos(freqs)[None, :, None, :]
            sin = jnp.sin(freqs)[None, :, None, :]
            x1, x2 = (x[..., :D // 2], x[..., D // 2:])
            out = jnp.concatenate([x1 * cos - x2 * sin, x1 * sin + x2 * cos], axis=-1)
            return out.astype(x.dtype)
        B, S, _ = hidden_states.shape
        q_size = N_HEADS * HEAD_DIM
        kv_size = N_KV_HEADS * HEAD_DIM
        qkv = hidden_states @ Wqkv
        xq = qkv[..., :q_size].reshape(B, S, N_HEADS, HEAD_DIM)
        xk = qkv[..., q_size:q_size + kv_size].reshape(B, S, N_KV_HEADS, HEAD_DIM)
        xv = qkv[..., q_size + kv_size:].reshape(B, S, N_KV_HEADS, HEAD_DIM)
        xq = apply_rotary_emb(xq)
        xk = apply_rotary_emb(xk)
        rep = N_HEADS // N_KV_HEADS
        xk = jnp.repeat(xk, rep, axis=2)
        xv = jnp.repeat(xv, rep, axis=2)
        logits = jnp.einsum('bqhd,bkhd->bhqk', xq, xk) * SCALE
        logits = SOFTCAP * jnp.tanh(logits / SOFTCAP)
        causal = jnp.tril(jnp.ones((S, S), dtype=bool))
        logits = jnp.where(causal[None, None], logits, jnp.float32(-1e+30))
        scores = jax.nn.softmax(logits, axis=-1)
        out = jnp.einsum('bhqk,bkhd->bqhd', scores, xv).reshape(B, S, N_HEADS * HEAD_DIM)
        return out @ Wo

    def _L0_xattn_ref(x, cond, mask, wq, bq, wk, bk, wv, bv, wo, bo):
        import jax, jax.numpy as jnp
        import numpy as np
        NUM_HEADS = 16
        EPS = 1e-08

        def _dyn_quant(x):
            s = jnp.maximum(jnp.max(jnp.abs(x), axis=-1, keepdims=True) / 127.0, EPS)
            q = jnp.clip(jnp.round(x / s), -127.0, 127.0)
            return (q, s)

        def _quant_weight(w):
            s = jnp.maximum(jnp.max(jnp.abs(w), axis=1, keepdims=True) / 127.0, EPS)
            q = jnp.clip(jnp.round(w / s), -127.0, 127.0)
            return (q, s)

        def _w8a8_linear(x, w, b):
            qx, sx = _dyn_quant(x)
            qw, sw = _quant_weight(w)
            y = jnp.einsum('bnc,oc->bno', qx, qw) * (sx * sw[:, 0])
            return y + b
        B, N, C = x.shape
        L = cond.shape[1]
        H = NUM_HEADS
        D = C // H
        inv_sqrt_d = np.float32(1.0 / np.sqrt(D))
        q = _w8a8_linear(x, wq, bq).reshape(B, N, H, D).transpose(0, 2, 1, 3)
        k = (cond @ wk.T + bk).reshape(B, L, H, D).transpose(0, 2, 1, 3)
        v = (cond @ wv.T + bv).reshape(B, L, H, D).transpose(0, 2, 1, 3)
        scores = jnp.einsum('bhnd,bhld->bhnl', q, k) * inv_sqrt_d + mask[:, None]
        attn = jax.nn.softmax(scores, axis=-1)
        o = jnp.einsum('bhnl,bhld->bhnd', attn, v)
        o = o.transpose(0, 2, 1, 3).reshape(B, N, C)
        return _w8a8_linear(o, wo, bo)

    def _L0_ffn_ref(x, Wr, br, W1, W2):
        import jax, jax.numpy as jnp
        import numpy as np
        N_BLOCKS = 16
        BLOCK_SIZE = 64
        TOP_K = N_BLOCKS // 4
        x_shape = x.shape
        in_f = x_shape[-1]
        xf = x.reshape(-1, in_f)
        n = xf.shape[0]
        prob = jax.nn.softmax(xf @ Wr.T + br, axis=-1)
        _, idx = jax.lax.top_k(prob, TOP_K)
        mask = jnp.zeros((n, N_BLOCKS), dtype=xf.dtype)
        mask = mask.at[jnp.arange(n)[:, None], idx].set(1.0)
        W1b = W1.reshape(N_BLOCKS, BLOCK_SIZE, in_f)
        h = jnp.einsum('nf,ibf->nib', xf, W1b)
        h = jax.nn.gelu(h, approximate=False) * mask[:, :, None]
        W2b = W2.reshape(in_f, N_BLOCKS, BLOCK_SIZE)
        y = jnp.einsum('nib,fib->nf', h, W2b)
        return y.reshape(x_shape)
    x = _layernorm(x + _L0_attn_ref(x, L0_attn_Wqkv, L0_attn_Wo), axis=-1)
    x = _layernorm(x + _L0_xattn_ref(x, ctx_2048, mask_BxSxS2_ff0, L0_xattn_wq, L0_xattn_bq, L0_xattn_wk, L0_xattn_bk, L0_xattn_wv, L0_xattn_bv, L0_xattn_wo, L0_xattn_bo), axis=-1)
    x = _layernorm(x + _L0_ffn_ref(x, L0_ffn_Wr, L0_ffn_br, L0_ffn_W1, L0_ffn_W2), axis=-1)
    return x

_drawn_inputs = setup_inputs


def setup_inputs(seed=0):
    import zlib

    import numpy as np

    out = dict(_drawn_inputs(seed))
    spreads = {'L0_xattn_bq': (0.0, 0.8),
     'L0_xattn_bk': (0.0, 0.8),
     'L0_xattn_bv': (0.0, 0.1),
     'L0_xattn_bo': (0.0, 0.1),
     'L0_ffn_br': (0.0, 0.1)}
    factors = {'L0_xattn_wq': 8.0, 'L0_xattn_wk': 5.937}
    for name, (base, spread) in spreads.items():
        noise = np.random.default_rng([zlib.crc32(name.encode()), seed]).standard_normal(out[name].shape)
        drawn = base * np.exp(spread * noise) if base else spread * noise
        out[name] = jnp.asarray(drawn.astype(out[name].dtype))
    for name, factor in factors.items():
        out[name] = (out[name] * factor).astype(out[name].dtype)
    return out
```

```python
from contextlib import ExitStack

import numpy as np

import concourse.bass as bass
from concourse import mybir

F32 = mybir.dt.float32
F32R = mybir.dt.float32r
BF16 = mybir.dt.bfloat16
ACT = mybir.ActivationFunctionType
ALU = mybir.AluOpType
AX_X = mybir.AxisListType.X

P = 128
B, T, C = 4, 256, 256
TT = T // P
CK = C // P
NH, NKV, HD = 16, 2, 128
PAIRS = NH // 2
QUADS = NH // 4
SCALE = 0.08838834764831845
SOFTCAP = 30.0
XH, XD = 16, C // 16
XPAIRS = XH // 2
XW = 2 * XD
NBLK, BLK, TOPK = 16, 64, 4
HID = NBLK * BLK
HT = HID // P
EPS_LN, EPS_Q, QMAX = 1e-5, 1e-8, 127.0
ROUND = 12582912.0
NBANK = 7
NEAR = 3
CONSTS = 12
PIECES = 5
PW = (NH + 2 * NKV) * HD // PIECES


def attention_ops(b):
    ops = [("split_x", b, 0), ("rot", b, 0), ("val", b, 0)]
    for s in range(PAIRS + 6):
        if s < PAIRS:
            ops.append(("rot", b, s + 1))
        j = s - 2
        if 0 <= j < PAIRS:
            ops.append(("near", b, j))
            if j % 2:
                ops.append(("far", b, j // 2))
        j = s - 4
        if 0 <= j < PAIRS:
            ops += [("mix", b, 2 * j), ("mix", b, 2 * j + 1)]
        if 0 <= j - 1 < PAIRS:
            ops.append(("turn", b, j - 1))
        if 0 <= j - 2 < PAIRS:
            ops.append(("proj", b, j - 2))
    ops.append(("norm1", b, 0))
    return ops


def rest_ops(b):
    ops = [("ctx", b, 0), ("ctx", b, 1), ("quant_x", b, 0), *(("turn_k", b, i) for i in range(QUADS)),
           ("turn_x", b, 0), ("query", b, 0), ("turn_q", b, 0)]
    for hp in range(XPAIRS + 1):
        if hp < XPAIRS:
            ops.append(("xscore", b, hp))
        if hp % 2 == 0 and hp + 2 < XPAIRS:
            ops.append(("turn_q", b, hp // 2 + 1))
        if hp >= 1:
            ops += [("turn_p", b, 2 * hp - 2), ("turn_p", b, 2 * hp - 1)]
            if hp % 2 == 0:
                ops.append(("xmix", b, hp // 2 - 1))
    ops += [("turn_o", b, 0), ("turn_o", b, 1), ("quant_o", b, 0), ("turn_ox", b, 0), ("outproj", b, 0),
            ("turn_z", b, 0), ("route", b, 0), ("turn_r", b, 0), ("turn_m", b, 0),
            ("hidden", b, 0), ("ffn", b, 0)]
    return ops


def merge(first, second):
    out, j = [], 0
    for i, op in enumerate(first):
        out.append(op)
        until = (i + 1) * len(second) // len(first)
        out += second[j:until]
        j = until
    return out


def make_plan():
    plan = []
    for op in attention_ops(0):
        kind, _, i = op
        if kind == "rot" and i == 0:
            plan += [("piece", 0, 0), ("piece", 0, 1)]
        if kind == "rot" and i % 2 and i < PAIRS - 1:
            plan.append(("piece", 0, (i + 3) // 2))
        if kind == "proj" and i == 0:
            plan += [("prep", 0, 0), ("prep", 0, 1)]
        plan.append(op)
    for b in range(B - 1):
        plan += merge(attention_ops(b + 1), rest_ops(b))
    return plan + rest_ops(B - 1)


BANKS = {"rot": 1, "val": 1, "near": 1, "far": 1, "mix": 1, "turn": 1, "ctx": 1, "turn_x": 1, "query": 1,
         "turn_k": 1, "turn_q": 1, "xscore": 2, "turn_p": 1, "xmix": 1, "turn_o": 1, "turn_ox": 1,
         "outproj": 1, "turn_z": 1, "route": 1, "turn_r": 1, "turn_m": 1, "hidden": HT, "ffn": 1,
         "prep": 2}
PER = {"x_hi": 1, "x_lo": 1, "roped": 3 * (PAIRS + 1), "rotated": PAIRS + 1, "values": 1,
       "capped": PAIRS + QUADS, "expd": PAIRS + QUADS, "causal": PAIRS + QUADS, "attn_rec": NH,
       "attn": NH, "attn_T": PAIRS, "projected": PAIRS,
       "ln1": 8, "ln2": 11, "ln3": 8, "rstd1": 1, "rstd2": 1, "rstd3": 1,
       "kv": 8, "quant_y": 7, "quant_o": 7, "y_T": 1, "query": 5, "k_T": QUADS, "q_T": QUADS,
       "xmasked": 5 * XPAIRS, "xexp": 4 * XPAIRS, "probs_T_even": XPAIRS, "probs_T_odd": XPAIRS,
       "xout": QUADS, "xattn": 2 * TT, "o_T": 1, "z_T": 1, "logits": 1, "route": 11, "route_exp": 1,
       "mask_T": 1, "gelu": HT // 2, "masked": HT // 2, "stored": 16}


def build_decoder(nc, x, xT, ctxT, mask, wqkv, wo, wkvT, xwq, xwo, xbias, wrT, br, w1T, w2T,
                  cos, sin, ident, out):
    plan = make_plan()
    where = {}
    n_uses = 0
    for kind, b, i in plan:
        for k in range(BANKS.get(kind, 0)):
            where[kind, b, i, k] = n_uses
            n_uses += 1
    used = sorted(where, key=where.get)

    with ExitStack() as ctx:
        def sb(name, shape, dt=F32, parts=P):
            return ctx.enter_context(nc.sbuf_tensor(name, [parts, *shape], dt))

        def sem(name):
            return ctx.enter_context(nc.semaphore(name))

        banks = [ctx.enter_context(nc.psum_tensor(f"bank{i}", [P, 512], F32)) for i in range(NBANK)]
        acc = ctx.enter_context(nc.psum_tensor("acc", [P, TT, C], F32))

        stage = sb("stage", [3, CK, PW])
        wq_hi = sb("wqkv_hi", [CK, PIECES * PW], F32R)
        wq_lo = sb("wqkv_lo", [CK, PIECES * PW], F32R)
        wo_s = sb("wo_s", [NH, C])
        wkv_s = sb("wkv_s", [CK, 2 * C])
        w1_s = sb("w1_s", [CK, HID])
        w2_s = sb("w2_s", [HT, C])
        wr_s = sb("wr_s", [CK, NBLK])
        br_s = sb("br_s", [1], parts=NBLK)
        xw_T = sb("xw_T", [2, CK, C], BF16)
        xw_scale = sb("xw_scale", [2, C])
        bias_s = sb("bias_s", [4, C])
        cos_s, sin_s = sb("cos_s", [T]), sb("sin_s", [T])
        ident_s = sb("ident_s", [P])
        identb_s = sb("identb_s", [P], BF16)
        ones = sb("ones", [P])
        pick_s = sb("pick_s", [HT, P], BF16, parts=NBLK)
        before_s = sb("before_s", [NBLK, NBLK], BF16)
        half = sb("half", [TT])

        xT_s, x_s = sb("xT_s", [CK, T]), sb("x_s", [TT, C])
        x_hi, x_lo = sb("x_hi", [CK, T], F32R), sb("x_lo", [CK, T], F32R)
        rope_t = sb("rope_t", [2, 2, T])
        q_T = sb("q_T", [4, 2, T])
        k_T = sb("k_T", [NKV, T])
        v_s = sb("v_s", [TT, NKV, HD + 1])
        p_near = sb("p_near", [NEAR, 2, T])
        p_far = sb("p_far", [2, 4, P])
        a_rec = sb("a_rec", [2, 2])
        a_s = sb("a_s", [2, TT, 2, HD])
        a_T = sb("a_T", [2, 2, T])
        y1 = sb("y1", [TT, C])

        ctx_s = sb("ctx_s", [CK, T])
        mask_s = sb("mask_s", [TT, T])
        parts = sb("parts", [TT, XH, 4, XD], F32R)
        kS = sb("kS", [QUADS, 2, T], F32R)
        qS = sb("qS", [2, 2, T], F32R)
        xv_s = sb("xv_s", [TT, XH, XW])
        xs = sb("xs", [2, 4, T])
        xmax, xneg = sb("xmax", [2, 4]), sb("xneg", [2, 4])
        xp_T = sb("xp_T", [2, 2, TT, T])
        xo_T = sb("xo_T", [QUADS, T])
        xrec = sb("xrec", [2, XH])
        q_tmp = sb("q_tmp", [TT, C])
        q_int = sb("q_int", [TT, C], BF16)
        q_intT = sb("q_intT", [CK, T], BF16)
        q_amax, q_scale, q_rs = sb("q_amax", [TT]), sb("q_scale", [TT]), sb("q_rs", [TT])
        z = sb("z", [TT, C])

        z_T = sb("z_T", [CK, T])
        lg_T = sb("lg_T", [T], parts=NBLK)
        r_max, r_sum, r_rec = sb("r_max", [TT]), sb("r_sum", [TT]), sb("r_rec", [TT])
        r_in, prob = sb("r_in", [TT, NBLK]), sb("prob", [TT, NBLK])
        above = sb("above", [TT, NBLK, NBLK], BF16)
        equal = sb("equal", [TT, NBLK, NBLK], BF16)
        rank = sb("rank", [TT, NBLK])
        keep = sb("keep", [TT, NBLK], BF16)
        keep_T = sb("keep_T", [T], BF16, parts=NBLK)
        flat = stage[:].rearrange("p a c n -> p (a c n)")
        g_T = flat[:, 0:HT * T].rearrange("p (t n) -> p t n", t=HT)
        h3, y3 = (flat[:, (HT + CK * n) * T:(HT + CK * (n + 1)) * T].rearrange("p (t c) -> p t c", t=TT)
                  for n in range(2))

        stats = [sb(f"stats{n}", [TT, 6]) for n in (1, 2, 3)]
        moments = [sb(f"moments{n}", [TT, 2]) for n in (1, 2, 3)]
        var_eps = [sb(f"var_eps{n}", [TT]) for n in (1, 2, 3)]
        rstd = [sb(f"rstd{n}", [TT]) for n in (1, 2, 3)]

        sig = {name: sem(name) for name in PER}
        filled = sem("filled")
        x_in, xtok_in, ctx_in, mask_in = sem("x_in"), sem("xtok_in"), sem("ctx_in"), sem("mask_in")
        piece_in = [sem(f"piece_in{i}") for i in range(PIECES)]
        tables_in, wkv_in, xw_in, xbias_in = sem("tables_in"), sem("wkv_in"), sem("xw_in"), sem("xbias_in")
        wo_in, ffn_in, route_in = sem("wo_in"), sem("ffn_in"), sem("route_in")
        piece_hi, piece_lo = sem("piece_hi"), sem("piece_lo")
        consts_set, bias_scaled = sem("consts_set"), sem("bias_scaled")
        quant_w, scale_diag, xw_T_done, xw_scale_done = (sem("quant_w"), sem("scale_diag"),
                                                         sem("xw_T_done"), sem("xw_scale_done"))

        def count(name, b, i=0):
            return b * PER[name] + i + 1

        def wait_for(eng, name, b, i=0):
            if b >= 0:
                eng.wait_ge(sig[name], count(name, b, i))

        def bank(kind, b, i=0, k=0):
            return banks[where[kind, b, i, k] % NBANK]

        def wait_filled(eng, kind, b, i=0, k=0):
            if b >= 0:
                eng.wait_ge(filled, where[kind, b, i, k] + 1)

        tiles = [(k, i) for k, b_, i in attention_ops(0) if k in ("near", "far")]
        tile_at = {t: n for n, t in enumerate(tiles)}

        def released(key):
            kind, b, i, k = key
            table = {
                "rot": ("roped", 3 * i + 2), "val": ("values", 0),
                "near": ("capped", tile_at.get(("near", i))), "far": ("capped", tile_at.get(("far", i))),
                "mix": ("attn", i), "turn": ("attn_T", i), "ctx": ("kv", 4 * i + 1), "turn_x": ("y_T", 0),
                "query": ("query", 1), "turn_k": ("k_T", i), "turn_q": ("q_T", i),
                "xscore": ("xmasked", 5 * i + 2 * k + 1),
                "turn_p": ("probs_T_odd" if i % 2 else "probs_T_even", i // 2), "xmix": ("xout", i),
                "turn_o": ("xattn", 2 * i + 1), "turn_ox": ("o_T", 0), "outproj": ("ln2", 1),
                "turn_z": ("z_T", 0), "route": ("logits", 0), "turn_r": ("route", 1), "turn_m": ("mask_T", 0),
                "hidden": ("gelu" if k % 2 == 0 else "masked", k // 2), "ffn": ("ln3", 0),
            }
            if kind == "prep":
                return (xw_T_done if k == 0 else xw_scale_done), i + 1
            name, n = table[kind]
            return sig[name], count(name, b, n)

        block = ctx.enter_context(nc.Block())

        @block.sync
        def _(sp):
            rows = lambda a: a.rearrange("(k p) n -> p k n", p=P)
            order = [PIECES - 1, *range(PIECES - 1)]

            def load_x(b):
                if b >= 1:
                    wait_for(sp, "x_lo", b - 1)
                sp.dma_start(xT_s[:], rows(xT[b])).then_inc(x_in, 16)

            def load_tokens(b):
                wait_for(sp, "ln1", b - 1, 7)
                sp.dma_start(x_s[:], rows(x[b])).then_inc(xtok_in, 16)

            def load_context(b):
                wait_filled(sp, "ctx", b - 1, 1)
                sp.dma_start(ctx_s[:], rows(ctxT[b])).then_inc(ctx_in, 16)

            def load_mask(b):
                wait_for(sp, "xmasked", b - 1, 5 * XPAIRS - 2)
                sp.dma_start(mask_s[:], rows(mask[b])).then_inc(mask_in, 16)

            load_x(0)
            sp.dma_start(stage[:, 0], rows(wqkv[:, order[0] * PW:(order[0] + 1) * PW])).then_inc(piece_in[0], 16)
            sp.dma_start(cos_s[:], cos).then_inc(tables_in, 16)
            sp.dma_start(sin_s[:], sin).then_inc(tables_in, 16)
            sp.dma_start(ident_s[:], ident).then_inc(tables_in, 16)
            for n, c in enumerate(order[1:], start=1):
                if n >= 3:
                    sp.wait_ge(piece_lo, n - 2)
                sp.dma_start(stage[:, n % 3], rows(wqkv[:, c * PW:(c + 1) * PW])).then_inc(piece_in[n], 16)
            sp.dma_start(wo_s[:], rows(wo)).then_inc(wo_in, 16)
            load_tokens(0)
            for w, a in enumerate((xwq, xwo)):
                sp.dma_start((z, y1)[w][:], rows(a)).then_inc(xw_in, 16)
            sp.dma_start(bias_s[:].rearrange("p a c -> p (a c)"), xbias.partition_broadcast(P)).then_inc(xbias_in, 16)
            sp.dma_start(wkv_s[:], rows(wkvT)).then_inc(wkv_in, 16)
            load_context(0)
            load_mask(0)
            load_x(1)
            sp.dma_start(w1_s[:], rows(w1T)).then_inc(ffn_in, 16)
            sp.dma_start(w2_s[:], rows(w2T)).then_inc(ffn_in, 16)
            sp.dma_start(wr_s[:], rows(wrT)).then_inc(route_in, 16)
            sp.dma_start(br_s[:], br).then_inc(route_in, 16)
            for b in range(B):
                if b + 1 < B:
                    load_tokens(b + 1)
                    load_context(b + 1)
                    if b + 2 < B:
                        load_x(b + 2)
                    load_mask(b + 1)
                wait_for(sp, "ln3", b, 7)
                sp.dma_start(rows(out[b]), y3).then_inc(sig["stored"], 16)
            sp.wait_ge(sig["stored"], 16 * B)

        @block.tensor
        def _(pe):
            mm, transpose = nc.tensor.matmul, nc.tensor.transpose

            def claim(kind, b, i=0, k=0):
                n = where[kind, b, i, k]
                if n >= NBANK:
                    pe.wait_ge(*released(used[n - NBANK]))
                return banks[n % NBANK]

            def three_pass(ps, lhs, rhs, k, last):
                for n, (i, j) in enumerate(((0, 0), (0, 1), (1, 0))):
                    ins = mm(ps, lhs[i], rhs[j], start=(k == 0 and n == 0), stop=(last and n == 2))
                return ins

            def rot(b, i):
                ps = claim("rot", b, i)
                wait_for(pe, "x_lo", b)
                pe.wait_ge(piece_lo, 1 if i == 0 else 2 + (i - 1) // 2)
                for m in range(2):
                    c0 = (NH + m if i == 0 else 2 * i - 2 + m) * HD
                    for k in range(CK):
                        w = [a[:, k, c0:c0 + HD] for a in (wq_hi, wq_lo)]
                        ins = three_pass(ps[:, m * T:(m + 1) * T], w, [x_hi[:, k, :], x_lo[:, k, :]], k, k == CK - 1)
                ins.then_inc(filled, 1)

            def val(b):
                ps = claim("val", b)
                wait_for(pe, "x_lo", b)
                c0 = (NH + NKV) * HD
                for t in range(TT):
                    for k in range(CK):
                        xk = [a[:, k, t * P:(t + 1) * P] for a in (x_hi, x_lo)]
                        w = [a[:, k, c0:c0 + NKV * HD] for a in (wq_hi, wq_lo)]
                        ins = three_pass(ps[:, t * C:(t + 1) * C], xk, w, k, k == CK - 1)
                ins.then_inc(filled, 1)

            def near(b, j):
                ps = claim("near", b, j)
                wait_for(pe, "rotated", b, j + 1)
                mm(ps[:, :], k_T[:, j // 4, 0:P], q_T[:, j % 4].rearrange("p h q -> p (h q)"),
                   start=True, stop=True).then_inc(filled, 1)

            def far(b, i):
                ps = claim("far", b, i)
                wait_for(pe, "rotated", b, 2 * i + 2)
                s = (2 * i) % 4
                mm(ps[:].rearrange("p (h q) -> p h q", h=4), k_T[:, i // 2, P:T],
                   q_T[:, s:s + 2, :, P:T].rearrange("p a h q -> p (a h) q"),
                   start=True, stop=True).then_inc(filled, 1)

            def mix(b, i):
                j, t = divmod(i, 2)
                ps = claim("mix", b, i)
                wait_for(pe, "values", b)
                wait_for(pe, "causal", b, tile_at["near", j])
                if t:
                    wait_for(pe, "causal", b, tile_at["far", j // 2])
                for m in range(2):
                    o = ps[:, m * (HD + 1):(m + 1) * (HD + 1)]
                    ins = mm(o, p_near[:, j % NEAR, m, t * P:(t + 1) * P], v_s[:, 0, j // 4, :],
                             start=True, stop=(t == 0))
                    if t:
                        ins = mm(o, p_far[:, (j // 2) % 2, 2 * (j % 2) + m, :], v_s[:, 1, j // 4, :],
                                 start=False, stop=True)
                ins.then_inc(filled, 1)

            def turn(b, j):
                ps = claim("turn", b, j)
                wait_for(pe, "attn", b, 2 * j + 1)
                for m in range(2):
                    for t in range(TT):
                        ins = transpose(ps[:, m * T + t * P:m * T + (t + 1) * P], a_s[:, j % 2, t, m, :], ident_s[:])
                ins.then_inc(filled, 1)

            def proj(b, j):
                wait_for(pe, "attn_T", b, j)
                if j == 0:
                    wait_for(pe, "ln1", b - 1, 0)
                    if b == 0:
                        pe.wait_ge(wo_in, 16)
                for t in range(TT):
                    for m in range(2):
                        ins = mm(acc[:, t, :], a_T[:, j % 2, m, t * P:(t + 1) * P], wo_s[:, 2 * j + m, :],
                                 start=(j == 0 and t == 0 and m == 0), stop=(j == PAIRS - 1 and m == 1),
                                 skip_group_check=True)
                ins.then_inc(sig["projected"], 1)

            def prep(i):
                ps = claim("prep", 0, i, 0)[:].bitcast(BF16)
                pe.wait_ge(quant_w, 7 * (i + 1))
                for k in range(CK):
                    for o in range(CK):
                        ins = transpose(ps[:, k * C + o * P:k * C + (o + 1) * P], q_int[:, o, k * P:(k + 1) * P],
                                        identb_s[:])
                ins.then_inc(filled, 1)
                ps = claim("prep", 0, i, 1)
                pe.wait_ge(scale_diag, CK * (i + 1))
                for o in range(CK):
                    ins = mm(ps[:, o * P:(o + 1) * P], ones[:], q_tmp[:, o, 0:P], start=True, stop=True)
                ins.then_inc(filled, 1)

            def context(b, t):
                ps = claim("ctx", b, t)
                pe.wait_ge(ctx_in, 16 * (b + 1))
                pe.wait_ge(wkv_in, 16)
                for k in range(CK):
                    ins = mm(ps[:, :], ctx_s[:, k, t * P:(t + 1) * P], wkv_s[:, k, :], start=(k == 0), stop=(k == CK - 1))
                ins.then_inc(filled, 1)

            def turn_ints(kind, b, signal):
                ps = claim(kind, b)[:].bitcast(BF16)
                wait_for(pe, signal, b, 6)
                for k in range(CK):
                    for t in range(TT):
                        ins = transpose(ps[:, k * T + t * P:k * T + (t + 1) * P], q_int[:, t, k * P:(k + 1) * P],
                                        identb_s[:])
                ins.then_inc(filled, 1)

            def int_product(kind, b, signal, w):
                ps = claim(kind, b)
                wait_for(pe, signal, b)
                if b == 0:
                    pe.wait_ge(xw_T_done, w + 1)
                for t in range(TT):
                    for k in range(CK):
                        ins = mm(ps[:, t * C:(t + 1) * C], q_intT[:, k, t * P:(t + 1) * P], xw_T[:, w, k, :],
                                 start=(k == 0), stop=(k == CK - 1))
                ins.then_inc(filled, 1)

            def stack(kind, b, i):
                ps = claim(kind, b, i)
                if kind == "turn_k":
                    wait_for(pe, "kv", b, 7)
                else:
                    wait_for(pe, "query", b, 4)
                for m in range(2):
                    for t in range(TT):
                        a = parts[:, t, 4 * i + 2 * m:4 * i + 2 * m + 2].rearrange("p h l c -> p (h l c)")
                        ins = transpose(ps[:, m * T + t * P:m * T + (t + 1) * P], a.bitcast(F32), ident_s[:])
                ins.then_inc(filled, 1)

            def xscore(b, hp):
                ps = [claim("xscore", b, hp, m) for m in range(2)]
                wait_for(pe, "k_T", b, hp // 2)
                wait_for(pe, "q_T", b, hp // 2)
                s, m2 = (hp // 2) % 2, hp % 2
                for t in range(TT):
                    for m in range(2):
                        r = slice(64 * m, 64 * m + 64)
                        ins = mm(ps[m][:, t * T:(t + 1) * T], qS[r, s, m2, t * P:(t + 1) * P], kS[r, hp // 2, m2, :],
                                 start=True, stop=True)
                        if t == TT - 1:
                            ins.then_inc(filled, 1)

            def turn_p(b, h):
                ps = claim("turn_p", b, h)
                hp, m = divmod(h, 2)
                wait_for(pe, "xexp", b, 4 * hp + 2 * m + 1)
                for k in range(TT):
                    for t in range(TT):
                        ins = transpose(ps[:, k * T + t * P:k * T + (t + 1) * P],
                                        xs[:, hp % 2, 2 * m + t, k * P:(k + 1) * P], ident_s[:])
                ins.then_inc(filled, 1)

            def xmix(b, g):
                ps = claim("xmix", b, g)
                wait_for(pe, "probs_T_even", b, 2 * g + 1)
                wait_for(pe, "probs_T_odd", b, 2 * g + 1)
                wait_for(pe, "kv", b, 5)
                for k in range(TT):
                    for m in range(4):
                        ins = mm(ps[XW * m:XW * (m + 1), 0:T], xv_s[:, k, 4 * g + m, :], xp_T[:, m // 2, m % 2, k, :],
                                 start=(k == 0), stop=(k == TT - 1))
                ins.then_inc(filled, 1)

            def turn_o(b, t):
                ps = claim("turn_o", b, t)
                wait_for(pe, "xout", b, QUADS - 1)
                for g in range(QUADS):
                    ins = transpose(ps[:, g * P:(g + 1) * P], xo_T[:, g, t * P:(t + 1) * P], ident_s[:])
                ins.then_inc(filled, 1)

            def turn_z(b):
                ps = claim("turn_z", b)
                wait_for(pe, "ln2", b, 10)
                for k in range(CK):
                    for t in range(TT):
                        ins = transpose(ps[:, k * T + t * P:k * T + (t + 1) * P], z[:, t, k * P:(k + 1) * P], ident_s[:])
                ins.then_inc(filled, 1)

            def route(b):
                ps = claim("route", b)
                wait_for(pe, "z_T", b)
                if b == 0:
                    pe.wait_ge(route_in, 32)
                for k in range(CK):
                    ins = mm(ps[0:NBLK, 0:T], wr_s[:, k, :], z_T[:, k, :], start=(k == 0), stop=(k == CK - 1))
                ins.then_inc(filled, 1)

            def turn_r(b):
                ps = claim("turn_r", b)
                wait_for(pe, "logits", b)
                for t in range(TT):
                    ins = transpose(ps[:, t * NBLK:(t + 1) * NBLK], lg_T[:, t * P:(t + 1) * P],
                                    ident_s[0:NBLK, 0:NBLK])
                ins.then_inc(filled, 1)

            def turn_m(b):
                ps = claim("turn_m", b)[:].bitcast(BF16)
                wait_for(pe, "route", b, 10)
                for t in range(TT):
                    ins = transpose(ps[0:NBLK, t * P:(t + 1) * P], keep[:, t, :], identb_s[:])
                ins.then_inc(filled, 1)

            def hidden(b):
                if b == 0:
                    pe.wait_ge(ffn_in, 32)
                for i in range(HT // 2):
                    ps = claim("hidden", b, 0, 2 * i)
                    for m in range(2):
                        for k in range(CK):
                            ins = mm(ps[:, m * T:(m + 1) * T], w1_s[:, k, (2 * i + m) * P:(2 * i + m + 1) * P],
                                     z_T[:, k, :], start=(k == 0), stop=(k == CK - 1))
                    ins.then_inc(filled, 1)
                    ps = claim("hidden", b, 0, 2 * i + 1)
                    wait_for(pe, "mask_T", b)
                    for m in range(2):
                        ins = mm(ps[:, m * T:(m + 1) * T], pick_s[:, 2 * i + m, :], keep_T[:], start=True, stop=True)
                    ins.then_inc(filled, 1)

            def ffn(b):
                ps = claim("ffn", b)
                wait_for(pe, "masked", b, HT // 2 - 1)
                for t in range(TT):
                    for n in range(HT):
                        ins = mm(ps[:, t * C:(t + 1) * C], g_T[:, n, t * P:(t + 1) * P], w2_s[:, n, :],
                                 start=(n == 0), stop=(n == HT - 1))
                ins.then_inc(filled, 1)

            pe.wait_ge(tables_in, 48)
            pe.wait_ge(consts_set, CONSTS)
            for kind, b, i in plan:
                if kind == "rot":
                    rot(b, i)
                elif kind == "val":
                    val(b)
                elif kind == "near":
                    near(b, i)
                elif kind == "far":
                    far(b, i)
                elif kind == "mix":
                    mix(b, i)
                elif kind == "turn":
                    turn(b, i)
                elif kind == "proj":
                    proj(b, i)
                elif kind == "prep":
                    prep(i)
                elif kind == "ctx":
                    context(b, i)
                elif kind == "turn_x":
                    turn_ints(kind, b, "quant_y")
                elif kind == "query":
                    int_product(kind, b, "y_T", 0)
                elif kind in ("turn_k", "turn_q"):
                    stack(kind, b, i)
                elif kind == "xscore":
                    xscore(b, i)
                elif kind == "turn_p":
                    turn_p(b, i)
                elif kind == "xmix":
                    xmix(b, i)
                elif kind == "turn_o":
                    turn_o(b, i)
                elif kind == "turn_ox":
                    turn_ints(kind, b, "quant_o")
                elif kind == "outproj":
                    int_product(kind, b, "o_T", 1)
                elif kind == "turn_z":
                    turn_z(b)
                elif kind == "route":
                    route(b)
                elif kind == "turn_r":
                    turn_r(b)
                elif kind == "turn_m":
                    turn_m(b)
                elif kind == "hidden":
                    hidden(b)
                elif kind == "ffn":
                    ffn(b)

        @block.scalar
        def _(act):
            activation, copy = nc.scalar.activation, nc.scalar.copy

            def evacuate(dst, src, kind, b, i, k, name):
                wait_filled(act, kind, b, i, k)
                copy(dst, src).then_inc(sig[name], 1)

            def split_piece(n):
                act.wait_ge(piece_in[n], 16)
                c = PIECES - 1 if n == 0 else n - 1
                copy(wq_hi[:, :, c * PW:(c + 1) * PW], stage[:, n % 3]).then_inc(piece_hi, 1)

            def split_x(b):
                act.wait_ge(x_in, 16 * (b + 1))
                wait_filled(act, "rot", b - 1, PAIRS)
                copy(x_hi[:], xT_s[:]).then_inc(sig["x_hi"], 1)

            def val(b):
                wait_filled(act, "val", b)
                wait_filled(act, "mix", b - 1, NH - 1)
                copy(v_s[:, :, :, 0:HD], bank("val", b)[:].rearrange("p (t g d) -> p t g d", t=TT, g=NKV))\
                    .then_inc(sig["values"], 1)

            def score(kind, b, i):
                n = tile_at[kind, i]
                if kind == "near":
                    dst = p_near[:, i % NEAR].rearrange("p h q -> p (h q)")
                    prev = (b, 2 * (i - NEAR) + 1) if i >= NEAR else (b - 1, 2 * range(i, PAIRS, NEAR)[-1] + 1)
                else:
                    dst = p_far[:, i % 2].rearrange("p h q -> p (h q)")
                    prev = (b, 4 * (i - 2) + 3) if i >= 2 else (b - 1, 4 * (i + QUADS - 2) + 3)
                wait_filled(act, "mix", *prev)
                wait_filled(act, kind, b, i)
                activation(dst, bank(kind, b, i)[:], ACT.Tanh, scale=SCALE / SOFTCAP).then_inc(sig["capped"], 1)
                wait_for(act, "capped", b, n)
                activation(dst, dst, ACT.Exp, scale=SOFTCAP).then_inc(sig["expd"], 1)

            def turn(b, j):
                if j < 2:
                    wait_for(act, "projected", b - 1, PAIRS - 2 + j)
                else:
                    wait_for(act, "projected", b, j - 2)
                evacuate(a_T[:, j % 2].rearrange("p h q -> p (h q)"), bank("turn", b, j)[:], "turn", b, j, 0, "attn_T")

            def prep(i):
                act.wait_ge(filled, where["prep", 0, i, 0] + 1)
                copy(xw_T[:, i].rearrange("p k c -> p (k c)"), bank("prep", 0, i, 0)[:].bitcast(BF16)[:, 0:CK * C])\
                    .then_inc(xw_T_done, 1)

            def stack(kind, b, i, dst, slots, name):
                if i >= slots:
                    wait_filled(act, "xscore", b, 2 * (i - slots) + 1, 1)
                else:
                    wait_filled(act, "xscore", b - 1, 2 * (i - slots + QUADS) + 1, 1)
                evacuate(dst[:, i % slots].rearrange("p a q -> p (a q)"), bank(kind, b, i)[:], kind, b, i, 0, name)

            def xexp(b, hp):
                for n in range(4):
                    wait_for(act, "xmasked", b, 5 * hp + 4)
                    activation(xs[:, hp % 2, n, :], xs[:, hp % 2, n, :], ACT.Exp, bias=xneg[:, hp % 2, n:n + 1])\
                        .then_inc(sig["xexp"], 1)

            def turn_p(b, h):
                if h % 2 == 0:
                    g = h // 4
                    wait_filled(act, "xmix", b if g else b - 1, g - 1 if g else QUADS - 1)
                    evacuate(xp_T[:, (h // 2) % 2, 0].rearrange("p k q -> p (k q)"), bank("turn_p", b, h)[:],
                             "turn_p", b, h, 0, "probs_T_even")

            def route_exp(b):
                wait_for(act, "route", b, 1)
                activation(prob[:], r_in[:], ACT.Exp).then_inc(sig["route_exp"], 1)

            def hidden(b):
                wait_filled(act, "ffn", b - 1)
                for i in range(HT // 2):
                    wait_filled(act, "hidden", b, 0, 2 * i)
                    activation(g_T[:, 2 * i:2 * i + 2, :].rearrange("p t n -> p (t n)"),
                               bank("hidden", b, 0, 2 * i)[:], ACT.Gelu).then_inc(sig["gelu"], 1)

            for kind, b, i in plan:
                if kind == "split_x":
                    split_x(b)
                elif kind == "piece":
                    split_piece(i)
                elif kind == "val":
                    val(b)
                elif kind in ("near", "far"):
                    score(kind, b, i)
                elif kind == "turn":
                    turn(b, i)
                elif kind == "prep":
                    prep(i)
                elif kind == "turn_k":
                    stack(kind, b, i, kS, QUADS, "k_T")
                elif kind == "turn_q":
                    stack(kind, b, i, qS, 2, "q_T")
                elif kind == "xscore":
                    xexp(b, i)
                elif kind == "turn_p":
                    turn_p(b, i)
                elif kind == "turn_x":
                    evacuate(q_intT[:].rearrange("p k q -> p (k q)"), bank(kind, b)[:].bitcast(BF16)[:, 0:CK * T],
                             kind, b, 0, 0, "y_T")
                elif kind == "turn_ox":
                    evacuate(q_intT[:].rearrange("p k q -> p (k q)"), bank(kind, b)[:].bitcast(BF16)[:, 0:CK * T],
                             kind, b, 0, 0, "o_T")
                elif kind == "xmix":
                    wait_filled(act, "turn_o", b - 1, 1)
                    evacuate(xo_T[:, i, :], bank(kind, b, i)[:, 0:T], kind, b, i, 0, "xout")
                elif kind == "turn_z":
                    wait_filled(act, "hidden", b - 1, 0, HT - 1)
                    evacuate(z_T[:].rearrange("p k q -> p (k q)"), bank(kind, b)[:], kind, b, 0, 0, "z_T")
                elif kind == "route":
                    wait_filled(act, kind, b)
                    activation(lg_T[:], bank(kind, b)[0:NBLK, 0:T], ACT.Identity, bias=br_s[:])\
                        .then_inc(sig["logits"], 1)
                elif kind == "turn_r":
                    route_exp(b)
                elif kind == "turn_m":
                    evacuate(keep_T[:], bank(kind, b)[0:NBLK, :].bitcast(BF16)[:, 0:T], kind, b, 0, 0, "mask_T")
                elif kind == "hidden":
                    hidden(b)

        @block.vector
        def _(dve):
            v = nc.vector

            def steps(semaphore, base):
                n = [base]

                def do(ins):
                    ins.then_inc(semaphore, 1)
                    n[0] += 1

                def done():
                    dve.wait_ge(semaphore, n[0])
                return do, done

            def split_piece(n):
                dve.wait_ge(piece_hi, n + 1)
                c = PIECES - 1 if n == 0 else n - 1
                cols = slice(c * PW, (c + 1) * PW)
                v.tensor_tensor(wq_lo[:, :, cols], stage[:, n % 3], wq_hi[:, :, cols].bitcast(F32), ALU.subtract)\
                    .then_inc(piece_lo, 1)

            def split_x(b):
                wait_for(dve, "x_hi", b)
                v.tensor_tensor(x_lo[:], xT_s[:], x_hi[:].bitcast(F32), ALU.subtract).then_inc(sig["x_lo"], 1)

            def rope(b, i):
                ps = bank("rot", b, i)[:].rearrange("p (h q) -> p h q", h=2)
                n = b * (PAIRS + 1) + i
                if n >= 2:
                    dve.wait_ge(sig["rotated"], n - 1)
                if i == 0:
                    wait_filled(dve, "far", b - 1, QUADS - 1)
                    dst = k_T[:]
                else:
                    j = i - 1
                    wait_filled(dve, "far", *((b, (j - 4) // 2) if j >= 4 else (b - 1, (j + PAIRS - 4) // 2)))
                    dst = q_T[:, j % 4]
                wait_filled(dve, "rot", b, i)
                c, s = (a[:].unsqueeze(1).to_broadcast([P, 2, T]) for a in (cos_s, sin_s))
                v.tensor_tensor(dst, ps, c, ALU.mult).then_inc(sig["roped"], 1)
                lower, upper = slice(0, HD // 2), slice(HD // 2, HD)
                t = rope_t[:, n % 2]
                v.tensor_tensor(t[lower], ps[upper], s[upper], ALU.mult).then_inc(sig["roped"], 1)
                v.tensor_tensor(t[upper], ps[lower], s[lower], ALU.mult).then_inc(sig["roped"], 1)

            def mix(b, i):
                j, t = divmod(i, 2)
                wait_filled(dve, "mix", b, i)
                if j < 2:
                    wait_filled(dve, "turn", b - 1, PAIRS - 2 + j)
                else:
                    wait_filled(dve, "turn", b, j - 2)
                ps = bank("mix", b, i)[:, 0:2 * (HD + 1)].rearrange("p (h d) -> p h d", h=2)
                rec = a_rec[:, i % 2, :].unsqueeze(2)
                v.reciprocal(rec, ps[:, :, HD:HD + 1]).then_inc(sig["attn_rec"], 1)
                wait_for(dve, "attn_rec", b, i)
                v.tensor_tensor(a_s[:, j % 2, t], ps[:, :, 0:HD], rec.to_broadcast([P, 2, HD]), ALU.mult)\
                    .then_inc(sig["attn"], 1)

            def layer_norm(n, b, do, done, h, y):
                done()
                for t in range(TT):
                    do(v.bn_stats(stats[n][:, t, :], h[:, t, :]))
                done()
                for t in range(TT):
                    do(v.bn_aggr(moments[n][:, t, :], stats[n][:, t, :]))
                done()
                do(v.tensor_scalar(var_eps[n][:], moments[n][:, :, 1], EPS_LN, None, ALU.add))
                dve.wait_ge(sig[f"rstd{n + 1}"], b + 1)
                for t in range(TT):
                    do(v.tensor_scalar(y[:, t, :], h[:, t, :], moments[n][:, t, 0:1], rstd[n][:, t:t + 1],
                                       ALU.subtract, ALU.mult))

            def norm1(b):
                wait_for(dve, "projected", b, PAIRS - 1)
                dve.wait_ge(xtok_in, 16 * (b + 1))
                do, done = steps(sig["ln1"], b * PER["ln1"])
                do(v.tensor_tensor(x_s[:], acc[:], x_s[:], ALU.add))
                wait_for(dve, "ln2", b - 1, 3)
                layer_norm(0, b, do, done, x_s, y1)

            def quantise(src, do, done):
                do(v.tensor_reduce(q_amax[:], src[:], AX_X, ALU.max, apply_absolute_value=True))
                done()
                do(v.tensor_scalar(q_scale[:], q_amax[:], 1.0 / QMAX, EPS_Q, ALU.mult, ALU.max))
                done()
                do(v.reciprocal(q_rs[:], q_scale[:]))
                done()
                for t in range(TT):
                    do(v.tensor_scalar(q_tmp[:, t, :], src[:, t, :], q_rs[:, t:t + 1], QMAX, ALU.mult, ALU.min))
                done()
                do(v.tensor_scalar(q_tmp[:], q_tmp[:], -QMAX, ROUND, ALU.max, ALU.add))
                done()
                do(v.tensor_scalar(q_int[:], q_tmp[:], ROUND, None, ALU.subtract))

            def prep(i):
                src = (z, y1)[i]
                dve.wait_ge(xw_in, 32)
                do, done = steps(quant_w, 7 * i)
                if i:
                    dve.wait_ge(filled, where["prep", 0, 0, 1] + 1)
                quantise(src, do, done)
                done()
                for o in range(CK):
                    v.tensor_scalar(q_tmp[:, o, 0:P], ident_s[:], q_scale[:, o:o + 1], None, ALU.mult)\
                        .then_inc(scale_diag, 1)
                factor = XD ** -0.5 if i == 0 else 1.0
                dve.wait_ge(filled, where["prep", 0, i, 1] + 1)
                v.tensor_scalar(xw_scale[:, i, :], bank("prep", 0, i, 1)[:, 0:C], factor, None, ALU.mult)\
                    .then_inc(xw_scale_done, 1)
                if i == 0:
                    dve.wait_ge(xbias_in, 16)
                    v.tensor_scalar(bias_s[:, 0, :], bias_s[:, 0, :], factor, None, ALU.mult).then_inc(bias_scaled, 1)

            def context(b, t):
                do, done = steps(sig["kv"], b * PER["kv"] + 4 * t)
                wait_filled(dve, "ctx", b, t)
                if t == 0:
                    wait_filled(dve, "xmix", b - 1, QUADS - 1)
                    wait_filled(dve, "turn_q", b - 1, QUADS - 1)
                    if b == 0:
                        dve.wait_ge(xbias_in, 16)
                        dve.wait_ge(filled, where["prep", 0, 1, 1] + 1)
                ps = bank("ctx", b, t)
                do(v.tensor_tensor(q_tmp[:, t, :], ps[:, 0:C], bias_s[:, 1, :], ALU.add))
                do(v.tensor_tensor(xv_s[:, t, :, 0:XD], ps[:, C:2 * C].rearrange("p (h c) -> p h c", h=XH),
                                   bias_s[:, 2, :].rearrange("p (h c) -> p h c", h=XH), ALU.add))
                done()
                k = q_tmp[:, t, :].rearrange("p (h c) -> p h c", h=XH).unsqueeze(2).to_broadcast([P, XH, 2, XD])
                do(v.tensor_copy(parts[:, t, :, 0:4:2, :], k))
                done()
                do(v.tensor_tensor(parts[:, t, :, 1:4:2, :], k, parts[:, t, :, 0:4:2, :].bitcast(F32), ALU.subtract))

            def quant_x(b):
                wait_filled(dve, "turn_ox", b - 1)
                if b == 0:
                    dve.wait_ge(filled, where["prep", 0, 1, 0] + 1)
                do, done = steps(sig["quant_y"], b * PER["quant_y"])
                wait_for(dve, "ln1", b, 7)
                quantise(y1, do, done)

            def dequantise(ps, w, do):
                for t in range(TT):
                    do(v.scalar_tensor_tensor(q_tmp[:, t, :], ps[:, t * C:(t + 1) * C], q_scale[:, t:t + 1],
                                              xw_scale[:, w, :], ALU.mult, ALU.mult))

            def query(b):
                wait_filled(dve, "query", b)
                if b == 0:
                    dve.wait_ge(xw_scale_done, 2)
                    dve.wait_ge(bias_scaled, 1)
                do, done = steps(sig["query"], b * PER["query"])
                dequantise(bank("query", b), 0, do)
                done()
                do(v.tensor_tensor(q_tmp[:], q_tmp[:], bias_s[:, 0:1, :].to_broadcast([P, TT, C]), ALU.add))
                done()
                wait_filled(dve, "turn_k", b, QUADS - 1)
                q = q_tmp[:].rearrange("p t (h c) -> p (t h) c", h=XH).unsqueeze(2).to_broadcast([P, TT * XH, 2, XD])
                qp = parts[:].rearrange("p t h l c -> p (t h) l c")
                do(v.tensor_copy(qp[:, :, 0:2, :], q))
                done()
                do(v.tensor_tensor(qp[:, :, 2:4, :], q, qp[:, :, 0:2, :].bitcast(F32), ALU.subtract))

            def xscore(b, hp):
                do, done = steps(sig["xmasked"], b * PER["xmasked"] + 5 * hp)
                if hp >= 2:
                    wait_filled(dve, "turn_p", b, 2 * hp - 3)
                else:
                    wait_filled(dve, "turn_p", b - 1, 2 * (hp + XPAIRS) - 3)
                if hp == 0:
                    dve.wait_ge(mask_in, 16 * (b + 1))
                s = hp % 2
                for m in range(2):
                    wait_filled(dve, "xscore", b, hp, m)
                    for t in range(TT):
                        n = 2 * m + t
                        do(v.tensor_tensor_reduce(out=xs[:, s, n, :], in0=bank("xscore", b, hp, m)[:, t * T:(t + 1) * T],
                                                  in1=mask_s[:, t, :], scale=1.0, scalar=-3.0e38, op0=ALU.add,
                                                  op1=ALU.max, accum_out=xmax[:, s, n:n + 1]))
                done()
                do(v.tensor_scalar(xneg[:, s, :], xmax[:, s, :], -1.0, None, ALU.mult))

            def turn_p(b, h):
                if h % 2:
                    g = h // 4
                    wait_filled(dve, "xmix", b if g else b - 1, g - 1 if g else QUADS - 1)
                    wait_filled(dve, "turn_p", b, h)
                    v.tensor_copy(xp_T[:, (h // 2) % 2, 1].rearrange("p k q -> p (k q)"), bank("turn_p", b, h)[:])\
                        .then_inc(sig["probs_T_odd"], 1)

            def turn_o(b, t):
                wait_filled(dve, "turn_o", b, t)
                ps = bank("turn_o", b, t)[:].rearrange("p (h w) -> p h w", w=XW)
                rec = xrec[:, t, :].unsqueeze(2)
                v.reciprocal(rec, ps[:, :, XD:XD + 1]).then_inc(sig["xattn"], 1)
                wait_for(dve, "xattn", b, 2 * t)
                v.tensor_tensor(q_tmp[:, t, :].rearrange("p (h c) -> p h c", h=XH), ps[:, :, 0:XD],
                                rec.to_broadcast([P, XH, XD]), ALU.mult).then_inc(sig["xattn"], 1)

            def quant_o(b):
                do, done = steps(sig["quant_o"], b * PER["quant_o"])
                wait_for(dve, "xattn", b, 2 * TT - 1)
                wait_for(dve, "query", b, 4)
                quantise(q_tmp, do, done)

            def outproj(b):
                wait_filled(dve, "outproj", b)
                do, done = steps(sig["ln2"], b * PER["ln2"])
                dequantise(bank("outproj", b), 1, do)
                done()
                do(v.tensor_tensor(q_tmp[:], q_tmp[:], bias_s[:, 3:4, :].to_broadcast([P, TT, C]), ALU.add))
                done()
                do(v.tensor_tensor(q_tmp[:], q_tmp[:], y1[:], ALU.add))
                wait_filled(dve, "turn_z", b - 1)
                wait_for(dve, "ln3", b - 1, 0)
                layer_norm(1, b, do, done, q_tmp, z)

            def router(b):
                do, done = steps(sig["route"], b * PER["route"])
                wait_filled(dve, "turn_r", b)
                ps = bank("turn_r", b)[:, 0:TT * NBLK].rearrange("p (t n) -> p t n", t=TT)
                wide = lambda a: a[:].unsqueeze(2).to_broadcast([P, TT, NBLK])
                do(v.tensor_reduce(r_max[:], ps, AX_X, ALU.max))
                done()
                do(v.tensor_tensor(r_in[:], ps, wide(r_max), ALU.subtract))
                wait_for(dve, "route_exp", b)
                do(v.tensor_reduce(r_sum[:], prob[:], AX_X, ALU.add))
                done()
                do(v.reciprocal(r_rec[:], r_sum[:]))
                done()
                do(v.tensor_tensor(prob[:], prob[:], wide(r_rec), ALU.mult))
                done()
                other = prob[:].unsqueeze(2).to_broadcast([P, TT, NBLK, NBLK])
                own = prob[:].unsqueeze(3).to_broadcast([P, TT, NBLK, NBLK])
                do(v.tensor_tensor(above[:], other, own, ALU.is_gt))
                do(v.tensor_tensor(equal[:], other, own, ALU.is_equal))
                done()
                if b == 0:
                    dve.wait_ge(consts_set, CONSTS)
                do(v.tensor_tensor(equal[:], equal[:], before_s[:].unsqueeze(1).to_broadcast([P, TT, NBLK, NBLK]),
                                   ALU.mult))
                done()
                do(v.tensor_tensor(above[:], above[:], equal[:], ALU.add))
                done()
                do(v.tensor_reduce(rank[:], above[:], AX_X, ALU.add))
                done()
                wait_filled(dve, "turn_m", b - 1)
                do(v.tensor_scalar(keep[:], rank[:], TOPK - 0.5, None, ALU.is_lt))

            def hidden(b):
                for i in range(HT // 2):
                    g = g_T[:, 2 * i:2 * i + 2, :].rearrange("p t n -> p (t n)")
                    wait_for(dve, "gelu", b, i)
                    wait_filled(dve, "hidden", b, 0, 2 * i + 1)
                    v.tensor_tensor(g, g, bank("hidden", b, 0, 2 * i + 1)[:], ALU.mult).then_inc(sig["masked"], 1)

            def ffn(b):
                wait_filled(dve, "ffn", b)
                do, done = steps(sig["ln3"], b * PER["ln3"])
                do(v.tensor_tensor(h3.rearrange("p t c -> p (t c)"), bank("ffn", b)[:],
                                   z[:].rearrange("p t c -> p (t c)"), ALU.add))
                if b:
                    dve.wait_ge(sig["stored"], 16 * b)
                layer_norm(2, b, do, done, h3, y3)

            dve.wait_ge(tables_in, 48)
            for kind, b, i in plan:
                if kind == "split_x":
                    split_x(b)
                elif kind == "piece":
                    split_piece(i)
                elif kind == "rot":
                    rope(b, i)
                elif kind == "mix":
                    mix(b, i)
                elif kind == "norm1":
                    norm1(b)
                elif kind == "prep":
                    prep(i)
                elif kind == "ctx":
                    context(b, i)
                elif kind == "quant_x":
                    quant_x(b)
                elif kind == "query":
                    query(b)
                elif kind == "xscore":
                    xscore(b, i)
                elif kind == "turn_p":
                    turn_p(b, i)
                elif kind == "turn_o":
                    turn_o(b, i)
                elif kind == "quant_o":
                    quant_o(b)
                elif kind == "outproj":
                    outproj(b)
                elif kind == "turn_r":
                    router(b)
                elif kind == "hidden":
                    hidden(b)
                elif kind == "ffn":
                    ffn(b)

        @block.gpsimd
        def _(pool):
            g = nc.gpsimd

            def constants():
                def select(out, pattern, base, channel, op):
                    g.affine_select(out=out, in_=out, compare_op=op, fill=0.0, base=base, pattern=pattern,
                                    channel_multiplier=channel).then_inc(consts_set, 1)

                g.memset(ones[:], 1.0).then_inc(consts_set, 1)
                g.memset(half[:], -0.5).then_inc(consts_set, 1)
                g.memset(v_s[:, :, :, HD:HD + 1], 1.0).then_inc(consts_set, 1)
                g.memset(xv_s[:, :, :, XD:XD + 1], 1.0).then_inc(consts_set, 1)
                g.memset(xv_s[:, :, :, XD + 1:XW], 0.0).then_inc(consts_set, 1)
                g.memset(identb_s[:], 1.0).then_inc(consts_set, 1)
                g.memset(pick_s[:], 1.0).then_inc(consts_set, 1)
                g.memset(before_s[:], 1.0).then_inc(consts_set, 1)
                pool.wait_ge(consts_set, 8)
                select(identb_s[:], [[-1, P]], 0, 1, ALU.is_equal)
                select(before_s[:], [[1, NBLK], [-1, NBLK]], 0, 0, ALU.is_gt)
                select(pick_s[:], [[P, HT], [1, P]], 0, -BLK, ALU.is_ge)
                pool.wait_ge(consts_set, 11)
                select(pick_s[:], [[-P, HT], [-1, P]], BLK - 1, BLK, ALU.is_ge)

            def rotate(b, i):
                n = b * (PAIRS + 1) + i
                dst = k_T[:] if i == 0 else q_T[:, (i - 1) % 4]
                wait_for(pool, "roped", b, 3 * i + 2)
                g.tensor_tensor(dst, dst, rope_t[:, n % 2], ALU.add).then_inc(sig["rotated"], 1)

            def causal(kind, b, i):
                wait_for(pool, "expd", b, tile_at[kind, i])
                p, heads = (p_near[:, i % NEAR, :, 0:P], 2) if kind == "near" else (p_far[:, i % 2], 4)
                g.affine_select(out=p, in_=p, compare_op=ALU.is_ge, fill=0.0, base=0,
                                pattern=[[0, heads], [1, P]], channel_multiplier=-1).then_inc(sig["causal"], 1)

            def inverse_root(n, b, name, step):
                wait_for(pool, name, b, step)
                g.tensor_tensor(rstd[n][:], var_eps[n][:], half[:], ALU.pow).then_inc(sig[f"rstd{n + 1}"], 1)

            constants()
            pool.wait_ge(consts_set, CONSTS)
            for kind, b, i in plan:
                if kind == "rot":
                    rotate(b, i)
                elif kind in ("near", "far"):
                    causal(kind, b, i)
                elif kind == "norm1":
                    inverse_root(0, b, "ln1", 5)
                elif kind == "outproj":
                    inverse_root(1, b, "ln2", 8)
                elif kind == "ffn":
                    inverse_root(2, b, "ln3", 5)


def rope_tables():
    freq = (np.float32(1.0) / np.float32(10000.0) ** (np.arange(0, HD, 2, dtype=np.float32) / np.float32(HD)))
    angle = np.outer(freq.astype(np.float32), np.arange(T, dtype=np.float32)).astype(np.float32)
    cos, sin = np.cos(angle), np.sin(angle)
    return np.concatenate([cos, cos]), np.concatenate([sin, -sin])


def kernel(**inputs):
    import concourse.bacc as bacc
    from concourse.bass_utils import run_bass_kernel_spmd

    a = {k: np.asarray(v) for k, v in inputs.items()}
    cos, sin = rope_tables()
    arrays = {
        "x": a["x"],
        "xT": a["x"].transpose(0, 2, 1),
        "ctxT": a["ctx_2048"].transpose(0, 2, 1),
        "mask": a["mask_BxSxS2_ff0"],
        "wqkv": a["L0_attn_Wqkv"],
        "wo": a["L0_attn_Wo"],
        "wkvT": np.concatenate([a["L0_xattn_wk"].T, a["L0_xattn_wv"].T], 1),
        "xwq": a["L0_xattn_wq"],
        "xwo": a["L0_xattn_wo"],
        "xbias": np.concatenate([a[f"L0_xattn_b{n}"] for n in "qkvo"]),
        "wrT": a["L0_ffn_Wr"].T,
        "br": a["L0_ffn_br"].reshape(NBLK, 1),
        "w1T": a["L0_ffn_W1"].T,
        "w2T": a["L0_ffn_W2"].T,
        "cos": cos,
        "sin": sin,
        "ident": np.eye(P, dtype=np.float32),
    }
    arrays = {f"in_{k}": np.ascontiguousarray(v) for k, v in arrays.items()}
    nc = bacc.Bacc("TRN2", target_bir_lowering=False, num_devices=1)
    args = [nc.dram_tensor(k, v.shape, mybir.dt.from_np(v.dtype), kind="ExternalInput").ap() for k, v in arrays.items()]
    out = nc.dram_tensor("out_y", (B, T, C), F32, kind="ExternalOutput").ap()
    build_decoder(nc, *args, out)
    r = run_bass_kernel_spmd(nc, [arrays], core_ids=[0])
    return r.results[0]["out_y"]
```

```python
from contextlib import ExitStack

import numpy as np

import concourse.bass as bass
from concourse import mybir

F32 = mybir.dt.float32
F32R = mybir.dt.float32r
BF16 = mybir.dt.bfloat16
ACT = mybir.ActivationFunctionType
ALU = mybir.AluOpType
AX_X = mybir.AxisListType.X

P = 128
B, T, C = 4, 256, 256
TT = T // P
CK = C // P
NH, NKV, HD = 16, 2, 128
PAIRS = NH // 2
QUADS = NH // 4
SCALE = 0.08838834764831845
SOFTCAP = 30.0
XH, XD = 16, C // 16
XPAIRS = XH // 2
XW = 2 * XD
NBLK, BLK, TOPK = 16, 64, 4
HID = NBLK * BLK
HT = HID // P
EPS_LN, EPS_Q, QMAX = 1e-5, 1e-8, 127.0
ROUND = 12582912.0
NBANK = 7
NEAR = 3
CONSTS = 12
HPARTS = 2
PIECES = 5
PW = (NH + 2 * NKV) * HD // PIECES


def attention_ops(b):
    ops = [("split_x", b, 0), ("rot", b, 0), ("val", b, 0)]
    for s in range(PAIRS + 6):
        if s < PAIRS:
            ops.append(("rot", b, s + 1))
        j = s - 2
        if 0 <= j < PAIRS:
            ops.append(("near", b, j))
            if j % 2:
                ops.append(("far", b, j // 2))
        j = s - 4
        if 0 <= j < PAIRS:
            ops += [("mix", b, 2 * j), ("mix", b, 2 * j + 1)]
        if 0 <= j - 1 < PAIRS:
            ops.append(("turn", b, j - 1))
        if 0 <= j - 2 < PAIRS:
            ops.append(("proj", b, j - 2))
    return ops + [("norm1", b, 0)]


def cross_ops(b):
    ops = [("ctx", b, 0), ("ctx", b, 1), *(("turn_k", b, i) for i in range(QUADS)),
           ("quant_x", b, 0), ("turn_x", b, 0), ("query", b, 0), ("turn_q", b, 0)]
    for hp in range(XPAIRS + 1):
        if hp < XPAIRS:
            ops.append(("xscore", b, hp))
        if hp % 2 == 0 and hp + 2 < XPAIRS:
            ops.append(("turn_q", b, hp // 2 + 1))
        if hp >= 3 and hp % 2:
            ops.append(("xmix", b, (hp - 3) // 2))
        if hp >= 1:
            ops += [("turn_p", b, 2 * hp - 2), ("turn_p", b, 2 * hp - 1)]
    return ops + [("xmix", b, QUADS - 1), ("turn_o", b, 0), ("turn_o", b, 1), ("quant_o", b, 0), ("turn_ox", b, 0), ("outproj", b, 0)]


def network_ops(b):
    return [("turn_z", b, 0), ("route", b, 0), ("turn_r", b, 0), ("turn_m", b, 0),
            *(("hidden", b, i) for i in range(HPARTS)), ("ffn", b, 0), ("ffn", b, 1)]


LENGTH = {"rot": 1.3, "val": 1.3, "near": 0.9, "far": 0.9, "mix": 0.65, "proj": 1.75, "ctx": 1.75,
          "xmix": 1.0, "route": 1.0, "hidden": 7.5 / HPARTS, "ffn": 3.5, "split_x": 0.0, "norm1": 0.0, "quant_x": 0.0,
          "quant_o": 0.0, "piece": 0.0}


def sources(op):
    kind, b, i = op
    table = {
        "rot": [("split_x", b, 0, 2.0)],
        "near": [("rot", b, i + 1, 5.0)],
        "far": [("rot", b, 2 * i + 2, 5.0)],
        "mix": [("near", b, i // 2, 3.5), ("far", b, i // 4, 3.5)] if i % 2 else [("near", b, i // 2, 3.5)],
        "turn": [("mix", b, 2 * i + 1, 1.5)],
        "proj": [("turn", b, i, 1.5)],
        "norm1": [("proj", b, PAIRS - 1, 0.5), ("outproj", b - 1, 0, 6.0)],
        "ctx": [("outproj", b - 1, 0, 3.0) if b else ("prep", 0, 1, 5.0)],
        "turn_k": [("ctx", b, 1, 5.0)],
        "quant_x": [("norm1", b, 0, 5.0)],
        "turn_x": [("quant_x", b, 0, 3.5)],
        "query": [("turn_x", b, 0, 1.5)],
        "turn_q": [("query", b, 0, 5.0)],
        "xscore": [("turn_q", b, i // 2, 1.5)],
        "turn_p": [("xscore", b, i // 2, 5.5)],
        "xmix": [("turn_p", b, 4 * i + 3, 1.5)],
        "turn_o": [("xmix", b, QUADS - 1, 1.0)],
        "quant_o": [("turn_o", b, 1, 1.5)],
        "turn_ox": [("quant_o", b, 0, 3.0)],
        "outproj": [("turn_ox", b, 0, 1.5), ("ffn", b - 1, 1, 1.0)],
        "turn_z": [("outproj", b, 0, 6.5)],
        "route": [("turn_z", b, 0, 1.5)],
        "turn_r": [("route", b, 0, 1.0)],
        "turn_m": [("turn_r", b, 0, 6.5)],
        "hidden": [("turn_m", b, 0, 0.5)],
        "ffn": [("hidden", b, HPARTS - 1, 2.0)],
    }
    return [((k, at, n), late) for k, at, n, late in table.get(kind, []) if at >= 0]


def make_plan():
    first = []
    for op in attention_ops(0):
        kind, _, i = op
        if kind == "rot" and i == 0:
            first += [("piece", 0, 0), ("piece", 0, 1)]
        if kind == "rot" and i % 2 and i < PAIRS - 1:
            first.append(("piece", 0, (i + 3) // 2))
        if kind == "turn" and i == PAIRS - 1:
            first += [("prep", 0, 0), ("prep", 0, 1)]
        first.append(op)
    streams = [[op for b in range(B) for op in cross_ops(b)],
               [op for b in range(B) for op in network_ops(b)],
               first + [op for b in range(1, B) for op in attention_ops(b)]]
    end, plan, now = {}, [], 0.0
    heads = streams[2]
    for b in range(B - 1):
        heads.remove(("norm1", b, 0))
        heads.insert(heads.index(("val", b + 1, 0)) + 1, ("norm1", b, 0))
    while any(streams):
        ready = []
        for rank, ops in enumerate(streams):
            if ops and all(source in end for source, _ in sources(ops[0])):
                at = max([end[source] + late for source, late in sources(ops[0])], default=0.0)
                ready.append((max(at, now), rank))
        at, rank = min(ready)
        op = streams[rank].pop(0)
        now = at + LENGTH.get(op[0], 0.45)
        end[op] = now
        plan.append(op)
    return plan


BANKS = {"rot": 1, "val": 1, "near": 1, "far": 1, "mix": 1, "turn": 1, "ctx": 1, "turn_x": 1, "query": 1,
         "turn_k": 1, "turn_q": 1, "xscore": 2, "turn_p": 1, "xmix": 1, "turn_o": 1, "turn_ox": 1,
         "outproj": 1, "turn_z": 1, "route": 1, "turn_r": 1, "turn_m": 1, "hidden": HT // HPARTS, "ffn": 1,
         "prep": 2}
PER = {"x_hi": 1, "x_lo": 1, "roped": 3 * (PAIRS + 1), "rotated": PAIRS + 1, "values": 1,
       "capped": PAIRS + QUADS, "expd": PAIRS + QUADS, "causal": PAIRS + QUADS, "attn_rec": NH,
       "attn": NH, "attn_T": PAIRS, "projected": PAIRS,
       "ln1": 8, "ln2": 11, "ln3": 5 * TT, "rstd1": 1, "rstd2": 1, "rstd3": TT,
       "kv": 8, "quant_y": 7, "quant_o": 7, "y_T": 1, "query": 5, "k_T": QUADS, "q_T": QUADS,
       "xmasked": 3 * XH, "xexp": 4 * XPAIRS, "probs_T_even": XPAIRS, "probs_T_odd": XPAIRS,
       "xout": QUADS, "xattn": 2 * TT, "o_T": 1, "z_T": 1, "logits": 1, "route": 11, "route_exp": 1,
       "mask_T": 1, "gelu": HT // 2, "masked": HT // 2, "stored": 16 * TT}


def build_decoder(nc, x, xT, ctxT, mask, wqkv, wo, wkvT, xwq, xwo, xbias, wrT, br, w1T, w2T,
                  cos, sin, ident, out):
    plan = make_plan()
    where = {}
    n_uses = 0
    for kind, b, i in plan:
        for k in range(BANKS.get(kind, 0)):
            where[kind, b, i, k] = n_uses
            n_uses += 1
    used = sorted(where, key=where.get)

    with ExitStack() as ctx:
        def sb(name, shape, dt=F32, parts=P):
            return ctx.enter_context(nc.sbuf_tensor(name, [parts, *shape], dt))

        def sem(name):
            return ctx.enter_context(nc.semaphore(name))

        banks = [ctx.enter_context(nc.psum_tensor(f"bank{i}", [P, 512], F32)) for i in range(NBANK)]
        acc = ctx.enter_context(nc.psum_tensor("acc", [P, TT, C], F32))

        stage = sb("stage", [3, CK, PW])
        wq_hi = sb("wqkv_hi", [CK, PIECES * PW], F32R)
        wq_lo = sb("wqkv_lo", [CK, PIECES * PW], F32R)
        wo_s = sb("wo_s", [NH, C])
        wkv_s = sb("wkv_s", [CK, 2 * C])
        w1_s = sb("w1_s", [CK, HID])
        w2_s = sb("w2_s", [HT, C])
        wr_s = sb("wr_s", [CK, NBLK])
        br_s = sb("br_s", [1], parts=NBLK)
        xw_T = sb("xw_T", [2, CK, C], BF16)
        xw_scale = sb("xw_scale", [2, C])
        bias_s = sb("bias_s", [4, C])
        cos_s, sin_s = sb("cos_s", [T]), sb("sin_s", [T])
        ident_s = sb("ident_s", [P])
        identb_s = sb("identb_s", [P], BF16)
        ones = sb("ones", [P])
        pick_s = sb("pick_s", [HT, P], BF16, parts=NBLK)
        before_s = sb("before_s", [NBLK, NBLK], BF16)
        half = sb("half", [TT])

        xT_s, x_s = sb("xT_s", [CK, T]), sb("x_s", [TT, C])
        x_hi, x_lo = sb("x_hi", [CK, T], F32R), sb("x_lo", [CK, T], F32R)
        rope_t = sb("rope_t", [2, 2, T])
        q_T = sb("q_T", [4, 2, T])
        k_T = sb("k_T", [NKV, T])
        v_s = sb("v_s", [TT, NKV, HD + 1])
        p_near = sb("p_near", [NEAR, 2, T])
        p_far = sb("p_far", [2, 4, P])
        a_rec = sb("a_rec", [2, 2])
        a_s = sb("a_s", [2, TT, 2, HD])
        a_T = sb("a_T", [2, 2, T])
        y1 = sb("y1", [TT, C])

        ctx_s = sb("ctx_s", [CK, T])
        mask_s = sb("mask_s", [TT, T])
        parts = sb("parts", [TT, XH, 4, XD], F32R)
        kS = sb("kS", [QUADS, 2, T], F32R)
        qS = sb("qS", [2, 2, T], F32R)
        xv_s = sb("xv_s", [TT, XH, XW])
        xs = sb("xs", [2, 4, T])
        xmax, xneg = sb("xmax", [2, 4]), sb("xneg", [2, 4])
        xp_T = sb("xp_T", [2, 2, TT, T])
        xo_T = sb("xo_T", [QUADS, T])
        xrec = sb("xrec", [2, XH])
        q_tmp = sb("q_tmp", [TT, C])
        q_int = sb("q_int", [TT, C], BF16)
        q_intT = sb("q_intT", [CK, T], BF16)
        q_amax, q_scale, q_rs = sb("q_amax", [TT]), sb("q_scale", [TT]), sb("q_rs", [TT])
        z = sb("z", [TT, C])

        z_T = sb("z_T", [CK, T])
        lg_T = sb("lg_T", [T], parts=NBLK)
        r_max, r_sum, r_rec = sb("r_max", [TT]), sb("r_sum", [TT]), sb("r_rec", [TT])
        r_in, prob = sb("r_in", [TT, NBLK]), sb("prob", [TT, NBLK])
        above = sb("above", [TT, NBLK, NBLK], BF16)
        equal = sb("equal", [TT, NBLK, NBLK], BF16)
        rank = sb("rank", [TT, NBLK])
        keep = sb("keep", [TT, NBLK], BF16)
        keep_T = sb("keep_T", [T], BF16, parts=NBLK)
        flat = stage[:].rearrange("p a c n -> p (a c n)")
        g_T = flat[:, 0:HT * T].rearrange("p (t n) -> p t n", t=HT)
        h3, y3 = (flat[:, (HT + CK * n) * T:(HT + CK * (n + 1)) * T].rearrange("p (t c) -> p t c", t=TT)
                  for n in range(2))

        stats = [sb(f"stats{n}", [TT, 6]) for n in (1, 2, 3)]
        moments = [sb(f"moments{n}", [TT, 2]) for n in (1, 2, 3)]
        var_eps = [sb(f"var_eps{n}", [TT]) for n in (1, 2, 3)]
        rstd = [sb(f"rstd{n}", [TT]) for n in (1, 2, 3)]

        sig = {name: sem(name) for name in PER}
        filled = sem("filled")
        x_in, xtok_in, ctx_in, mask_in = sem("x_in"), sem("xtok_in"), sem("ctx_in"), sem("mask_in")
        piece_in = [sem(f"piece_in{i}") for i in range(PIECES)]
        tables_in, wkv_in, xw_in, xbias_in = sem("tables_in"), sem("wkv_in"), sem("xw_in"), sem("xbias_in")
        wo_in, ffn_in, route_in = sem("wo_in"), sem("ffn_in"), sem("route_in")
        piece_hi, piece_lo = sem("piece_hi"), sem("piece_lo")
        consts_set, bias_scaled = sem("consts_set"), sem("bias_scaled")
        quant_w, scale_diag, xw_T_done, xw_scale_done = (sem("quant_w"), sem("scale_diag"),
                                                         sem("xw_T_done"), sem("xw_scale_done"))

        def count(name, b, i=0):
            return b * PER[name] + i + 1

        def wait_for(eng, name, b, i=0):
            if b >= 0:
                eng.wait_ge(sig[name], count(name, b, i))

        def bank(kind, b, i=0, k=0):
            return banks[where[kind, b, i, k] % NBANK]

        def wait_filled(eng, kind, b, i=0, k=0):
            if b >= 0:
                eng.wait_ge(filled, where[kind, b, i, k] + 1)

        tiles = [(k, i) for k, b_, i in attention_ops(0) if k in ("near", "far")]
        tile_at = {t: n for n, t in enumerate(tiles)}

        def released(key):
            kind, b, i, k = key
            table = {
                "rot": ("roped", 3 * i + 2), "val": ("values", 0),
                "near": ("capped", tile_at.get(("near", i))), "far": ("capped", tile_at.get(("far", i))),
                "mix": ("attn", i), "turn": ("attn_T", i), "ctx": ("kv", 4 * i + 1), "turn_x": ("y_T", 0),
                "query": ("query", 1), "turn_k": ("k_T", i), "turn_q": ("q_T", i),
                "xscore": ("xmasked", 3 * (2 * i + k) + 1),
                "turn_p": ("probs_T_odd" if i % 2 else "probs_T_even", i // 2), "xmix": ("xout", i),
                "turn_o": ("xattn", 2 * i + 1), "turn_ox": ("o_T", 0), "outproj": ("ln2", 1),
                "turn_z": ("z_T", 0), "route": ("logits", 0), "turn_r": ("route", 1), "turn_m": ("mask_T", 0),
                "hidden": ("gelu" if k % 2 == 0 else "masked", (i * BANKS["hidden"] + k) // 2),
                "ffn": ("ln3", 5 * i),
            }
            if kind == "prep":
                return (xw_T_done if k == 0 else xw_scale_done), i + 1
            name, n = table[kind]
            return sig[name], count(name, b, n)

        block = ctx.enter_context(nc.Block())

        @block.sync
        def _(sp):
            rows = lambda a: a.rearrange("(k p) n -> p k n", p=P)
            order = [PIECES - 1, *range(PIECES - 1)]

            def load_tokens(b):
                wait_for(sp, "ln1", b - 1, 7)
                sp.dma_start(x_s[:], rows(x[b])).then_inc(xtok_in, 16)

            def load_context(b):
                wait_filled(sp, "ctx", b - 1, 1)
                sp.dma_start(ctx_s[:], rows(ctxT[b])).then_inc(ctx_in, 16)

            def load_mask(b):
                wait_for(sp, "xmasked", b - 1, 3 * XH - 2)
                sp.dma_start(mask_s[:], rows(mask[b])).then_inc(mask_in, 16)

            sp.dma_start(xT_s[:], rows(xT[0])).then_inc(x_in, 16)
            sp.dma_start(stage[:, 0], rows(wqkv[:, order[0] * PW:(order[0] + 1) * PW])).then_inc(piece_in[0], 16)
            sp.dma_start(cos_s[:], cos).then_inc(tables_in, 16)
            sp.dma_start(sin_s[:], sin).then_inc(tables_in, 16)
            sp.dma_start(ident_s[:], ident).then_inc(tables_in, 16)
            for n, c in enumerate(order[1:], start=1):
                if n >= 3:
                    sp.wait_ge(piece_lo, n - 2)
                sp.dma_start(stage[:, n % 3], rows(wqkv[:, c * PW:(c + 1) * PW])).then_inc(piece_in[n], 16)
            sp.dma_start(wo_s[:], rows(wo)).then_inc(wo_in, 16)
            load_tokens(0)
            for w, a in enumerate((xwq, xwo)):
                sp.dma_start((z, y1)[w][:], rows(a)).then_inc(xw_in, 16)
            sp.dma_start(bias_s[:].rearrange("p a c -> p (a c)"), xbias.partition_broadcast(P)).then_inc(xbias_in, 16)
            sp.dma_start(wkv_s[:], rows(wkvT)).then_inc(wkv_in, 16)
            load_context(0)
            load_mask(0)
            sp.dma_start(w1_s[:], rows(w1T)).then_inc(ffn_in, 16)
            sp.dma_start(w2_s[:], rows(w2T)).then_inc(ffn_in, 16)
            sp.dma_start(wr_s[:], rows(wrT)).then_inc(route_in, 16)
            sp.dma_start(br_s[:], br).then_inc(route_in, 16)
            for b in range(B):
                if b + 1 < B:
                    load_tokens(b + 1)
                    load_context(b + 1)
                    load_mask(b + 1)
                for t in range(TT):
                    wait_for(sp, "ln3", b, 5 * t + 4)
                    sp.dma_start(out[b, t * P:(t + 1) * P, :], y3[:, t, :]).then_inc(sig["stored"], 16)
            sp.wait_ge(sig["stored"], 16 * TT * B)

        @block.tensor
        def _(pe):
            mm, transpose = nc.tensor.matmul, nc.tensor.transpose

            def claim(kind, b, i=0, k=0):
                n = where[kind, b, i, k]
                if n >= NBANK:
                    pe.wait_ge(*released(used[n - NBANK]))
                return banks[n % NBANK]

            def three_pass(ps, lhs, rhs, k, last):
                for n, (i, j) in enumerate(((0, 0), (0, 1), (1, 0))):
                    ins = mm(ps, lhs[i], rhs[j], start=(k == 0 and n == 0), stop=(last and n == 2))
                return ins

            def rot(b, i):
                ps = claim("rot", b, i)
                wait_for(pe, "x_lo", b)
                pe.wait_ge(piece_lo, 1 if i == 0 else 2 + (i - 1) // 2)
                for m in range(2):
                    c0 = (NH + m if i == 0 else 2 * i - 2 + m) * HD
                    for k in range(CK):
                        w = [a[:, k, c0:c0 + HD] for a in (wq_hi, wq_lo)]
                        ins = three_pass(ps[:, m * T:(m + 1) * T], w, [x_hi[:, k, :], x_lo[:, k, :]], k, k == CK - 1)
                ins.then_inc(filled, 1)

            def val(b):
                ps = claim("val", b)
                wait_for(pe, "x_lo", b)
                c0 = (NH + NKV) * HD
                for t in range(TT):
                    for k in range(CK):
                        xk = [a[:, k, t * P:(t + 1) * P] for a in (x_hi, x_lo)]
                        w = [a[:, k, c0:c0 + NKV * HD] for a in (wq_hi, wq_lo)]
                        ins = three_pass(ps[:, t * C:(t + 1) * C], xk, w, k, k == CK - 1)
                ins.then_inc(filled, 1)

            def near(b, j):
                ps = claim("near", b, j)
                wait_for(pe, "rotated", b, j + 1)
                mm(ps[:, :], k_T[:, j // 4, 0:P], q_T[:, j % 4].rearrange("p h q -> p (h q)"),
                   start=True, stop=True).then_inc(filled, 1)

            def far(b, i):
                ps = claim("far", b, i)
                wait_for(pe, "rotated", b, 2 * i + 2)
                s = (2 * i) % 4
                mm(ps[:].rearrange("p (h q) -> p h q", h=4), k_T[:, i // 2, P:T],
                   q_T[:, s:s + 2, :, P:T].rearrange("p a h q -> p (a h) q"),
                   start=True, stop=True).then_inc(filled, 1)

            def mix(b, i):
                j, t = divmod(i, 2)
                ps = claim("mix", b, i)
                wait_for(pe, "values", b)
                wait_for(pe, "causal", b, tile_at["near", j])
                if t:
                    wait_for(pe, "causal", b, tile_at["far", j // 2])
                for m in range(2):
                    o = ps[:, m * (HD + 1):(m + 1) * (HD + 1)]
                    ins = mm(o, p_near[:, j % NEAR, m, t * P:(t + 1) * P], v_s[:, 0, j // 4, :],
                             start=True, stop=(t == 0))
                    if t:
                        ins = mm(o, p_far[:, (j // 2) % 2, 2 * (j % 2) + m, :], v_s[:, 1, j // 4, :],
                                 start=False, stop=True)
                ins.then_inc(filled, 1)

            def turn(b, j):
                ps = claim("turn", b, j)
                wait_for(pe, "attn", b, 2 * j + 1)
                for m in range(2):
                    for t in range(TT):
                        ins = transpose(ps[:, m * T + t * P:m * T + (t + 1) * P], a_s[:, j % 2, t, m, :], ident_s[:])
                ins.then_inc(filled, 1)

            def proj(b, j):
                wait_for(pe, "attn_T", b, j)
                if j == 0:
                    wait_for(pe, "ln1", b - 1, 0)
                    if b == 0:
                        pe.wait_ge(wo_in, 16)
                for t in range(TT):
                    for m in range(2):
                        ins = mm(acc[:, t, :], a_T[:, j % 2, m, t * P:(t + 1) * P], wo_s[:, 2 * j + m, :],
                                 start=(j == 0 and t == 0 and m == 0), stop=(j == PAIRS - 1 and m == 1),
                                 skip_group_check=True)
                ins.then_inc(sig["projected"], 1)

            def prep(i):
                ps = claim("prep", 0, i, 0)[:].bitcast(BF16)
                pe.wait_ge(quant_w, 7 * (i + 1))
                for k in range(CK):
                    for o in range(CK):
                        ins = transpose(ps[:, k * C + o * P:k * C + (o + 1) * P], q_int[:, o, k * P:(k + 1) * P],
                                        identb_s[:])
                ins.then_inc(filled, 1)
                ps = claim("prep", 0, i, 1)
                pe.wait_ge(scale_diag, CK * (i + 1))
                for o in range(CK):
                    ins = mm(ps[:, o * P:(o + 1) * P], ones[:], q_tmp[:, o, 0:P], start=True, stop=True)
                ins.then_inc(filled, 1)

            def context(b, t):
                ps = claim("ctx", b, t)
                pe.wait_ge(ctx_in, 16 * (b + 1))
                pe.wait_ge(wkv_in, 16)
                for k in range(CK):
                    ins = mm(ps[:, :], ctx_s[:, k, t * P:(t + 1) * P], wkv_s[:, k, :], start=(k == 0), stop=(k == CK - 1))
                ins.then_inc(filled, 1)

            def turn_ints(kind, b, signal):
                ps = claim(kind, b)[:].bitcast(BF16)
                wait_for(pe, signal, b, 6)
                for k in range(CK):
                    for t in range(TT):
                        ins = transpose(ps[:, k * T + t * P:k * T + (t + 1) * P], q_int[:, t, k * P:(k + 1) * P],
                                        identb_s[:])
                ins.then_inc(filled, 1)

            def int_product(kind, b, signal, w):
                ps = claim(kind, b)
                wait_for(pe, signal, b)
                if b == 0:
                    pe.wait_ge(xw_T_done, w + 1)
                for t in range(TT):
                    for k in range(CK):
                        ins = mm(ps[:, t * C:(t + 1) * C], q_intT[:, k, t * P:(t + 1) * P], xw_T[:, w, k, :],
                                 start=(k == 0), stop=(k == CK - 1))
                ins.then_inc(filled, 1)

            def stack(kind, b, i):
                ps = claim(kind, b, i)
                if kind == "turn_k":
                    wait_for(pe, "kv", b, 7)
                else:
                    wait_for(pe, "query", b, 4)
                for m in range(2):
                    for t in range(TT):
                        a = parts[:, t, 4 * i + 2 * m:4 * i + 2 * m + 2].rearrange("p h l c -> p (h l c)")
                        ins = transpose(ps[:, m * T + t * P:m * T + (t + 1) * P], a.bitcast(F32), ident_s[:])
                ins.then_inc(filled, 1)

            def xscore(b, hp):
                ps = [claim("xscore", b, hp, m) for m in range(2)]
                wait_for(pe, "k_T", b, hp // 2)
                wait_for(pe, "q_T", b, hp // 2)
                s, m2 = (hp // 2) % 2, hp % 2
                for t in range(TT):
                    for m in range(2):
                        r = slice(64 * m, 64 * m + 64)
                        ins = mm(ps[m][:, t * T:(t + 1) * T], qS[r, s, m2, t * P:(t + 1) * P], kS[r, hp // 2, m2, :],
                                 start=True, stop=True)
                        if t == TT - 1:
                            ins.then_inc(filled, 1)

            def turn_p(b, h):
                ps = claim("turn_p", b, h)
                hp, m = divmod(h, 2)
                wait_for(pe, "xexp", b, 4 * hp + 2 * m + 1)
                for k in range(TT):
                    for t in range(TT):
                        ins = transpose(ps[:, k * T + t * P:k * T + (t + 1) * P],
                                        xs[:, hp % 2, 2 * m + t, k * P:(k + 1) * P], ident_s[:])
                ins.then_inc(filled, 1)

            def xmix(b, g):
                ps = claim("xmix", b, g)
                wait_for(pe, "probs_T_even", b, 2 * g + 1)
                wait_for(pe, "probs_T_odd", b, 2 * g + 1)
                wait_for(pe, "kv", b, 5)
                for k in range(TT):
                    for m in range(4):
                        ins = mm(ps[XW * m:XW * (m + 1), 0:T], xv_s[:, k, 4 * g + m, :], xp_T[:, m // 2, m % 2, k, :],
                                 start=(k == 0), stop=(k == TT - 1))
                ins.then_inc(filled, 1)

            def turn_o(b, t):
                ps = claim("turn_o", b, t)
                wait_for(pe, "xout", b, QUADS - 1)
                for g in range(QUADS):
                    ins = transpose(ps[:, g * P:(g + 1) * P], xo_T[:, g, t * P:(t + 1) * P], ident_s[:])
                ins.then_inc(filled, 1)

            def turn_z(b):
                ps = claim("turn_z", b)
                wait_for(pe, "ln2", b, 10)
                for k in range(CK):
                    for t in range(TT):
                        ins = transpose(ps[:, k * T + t * P:k * T + (t + 1) * P], z[:, t, k * P:(k + 1) * P], ident_s[:])
                ins.then_inc(filled, 1)

            def route(b):
                ps = claim("route", b)
                wait_for(pe, "z_T", b)
                if b == 0:
                    pe.wait_ge(route_in, 32)
                for k in range(CK):
                    ins = mm(ps[0:NBLK, 0:T], wr_s[:, k, :], z_T[:, k, :], start=(k == 0), stop=(k == CK - 1))
                ins.then_inc(filled, 1)

            def turn_r(b):
                ps = claim("turn_r", b)
                wait_for(pe, "logits", b)
                for t in range(TT):
                    ins = transpose(ps[:, t * NBLK:(t + 1) * NBLK], lg_T[:, t * P:(t + 1) * P],
                                    ident_s[0:NBLK, 0:NBLK])
                ins.then_inc(filled, 1)

            def turn_m(b):
                ps = claim("turn_m", b)[:].bitcast(BF16)
                wait_for(pe, "route", b, 10)
                for t in range(TT):
                    ins = transpose(ps[0:NBLK, t * P:(t + 1) * P], keep[:, t, :], identb_s[:])
                ins.then_inc(filled, 1)

            def hidden(b, part):
                if b == 0:
                    pe.wait_ge(ffn_in, 32)
                for n in range(HT // HPARTS // 2):
                    i = part * (HT // HPARTS // 2) + n
                    ps = claim("hidden", b, part, 2 * n)
                    for m in range(2):
                        for k in range(CK):
                            ins = mm(ps[:, m * T:(m + 1) * T], w1_s[:, k, (2 * i + m) * P:(2 * i + m + 1) * P],
                                     z_T[:, k, :], start=(k == 0), stop=(k == CK - 1))
                    ins.then_inc(filled, 1)
                    ps = claim("hidden", b, part, 2 * n + 1)
                    wait_for(pe, "mask_T", b)
                    for m in range(2):
                        ins = mm(ps[:, m * T:(m + 1) * T], pick_s[:, 2 * i + m, :], keep_T[:], start=True, stop=True)
                    ins.then_inc(filled, 1)

            def ffn(b, t):
                ps = claim("ffn", b, t)
                wait_for(pe, "masked", b, HT // 2 - 1)
                for n in range(HT):
                    ins = mm(ps[:, 0:C], g_T[:, n, t * P:(t + 1) * P], w2_s[:, n, :], start=(n == 0), stop=(n == HT - 1))
                ins.then_inc(filled, 1)

            pe.wait_ge(tables_in, 48)
            pe.wait_ge(consts_set, CONSTS)
            for kind, b, i in plan:
                if kind == "rot":
                    rot(b, i)
                elif kind == "val":
                    val(b)
                elif kind == "near":
                    near(b, i)
                elif kind == "far":
                    far(b, i)
                elif kind == "mix":
                    mix(b, i)
                elif kind == "turn":
                    turn(b, i)
                elif kind == "proj":
                    proj(b, i)
                elif kind == "prep":
                    prep(i)
                elif kind == "ctx":
                    context(b, i)
                elif kind == "turn_x":
                    turn_ints(kind, b, "quant_y")
                elif kind == "query":
                    int_product(kind, b, "y_T", 0)
                elif kind in ("turn_k", "turn_q"):
                    stack(kind, b, i)
                elif kind == "xscore":
                    xscore(b, i)
                elif kind == "turn_p":
                    turn_p(b, i)
                elif kind == "xmix":
                    xmix(b, i)
                elif kind == "turn_o":
                    turn_o(b, i)
                elif kind == "turn_ox":
                    turn_ints(kind, b, "quant_o")
                elif kind == "outproj":
                    int_product(kind, b, "o_T", 1)
                elif kind == "turn_z":
                    turn_z(b)
                elif kind == "route":
                    route(b)
                elif kind == "turn_r":
                    turn_r(b)
                elif kind == "turn_m":
                    turn_m(b)
                elif kind == "hidden":
                    hidden(b, i)
                elif kind == "ffn":
                    ffn(b, i)

        @block.scalar
        def _(act):
            activation, copy = nc.scalar.activation, nc.scalar.copy

            def evacuate(dst, src, kind, b, i, k, name):
                wait_filled(act, kind, b, i, k)
                copy(dst, src).then_inc(sig[name], 1)

            def split_piece(n):
                act.wait_ge(piece_in[n], 16)
                c = PIECES - 1 if n == 0 else n - 1
                copy(wq_hi[:, :, c * PW:(c + 1) * PW], stage[:, n % 3]).then_inc(piece_hi, 1)

            def split_x(b):
                act.wait_ge(x_in, 16 * (b + 1))
                wait_filled(act, "rot", b - 1, PAIRS)
                copy(x_hi[:], xT_s[:]).then_inc(sig["x_hi"], 1)

            def val(b):
                wait_filled(act, "val", b)
                wait_filled(act, "mix", b - 1, NH - 1)
                copy(v_s[:, :, :, 0:HD], bank("val", b)[:].rearrange("p (t g d) -> p t g d", t=TT, g=NKV))\
                    .then_inc(sig["values"], 1)
                if b + 1 < B:
                    wait_for(act, "x_lo", b)
                    act.dma_start(xT_s[:], xT[b + 1].rearrange("(k p) n -> p k n", p=P)).then_inc(x_in, 16)

            def score(kind, b, i):
                n = tile_at[kind, i]
                if kind == "near":
                    dst = p_near[:, i % NEAR].rearrange("p h q -> p (h q)")
                    prev = (b, 2 * (i - NEAR) + 1) if i >= NEAR else (b - 1, 2 * range(i, PAIRS, NEAR)[-1] + 1)
                else:
                    dst = p_far[:, i % 2].rearrange("p h q -> p (h q)")
                    prev = (b, 4 * (i - 2) + 3) if i >= 2 else (b - 1, 4 * (i + QUADS - 2) + 3)
                wait_filled(act, "mix", *prev)
                wait_filled(act, kind, b, i)
                activation(dst, bank(kind, b, i)[:], ACT.Tanh, scale=SCALE / SOFTCAP).then_inc(sig["capped"], 1)
                wait_for(act, "capped", b, n)
                activation(dst, dst, ACT.Exp, scale=SOFTCAP).then_inc(sig["expd"], 1)

            def turn(b, j):
                if j < 2:
                    wait_for(act, "projected", b - 1, PAIRS - 2 + j)
                else:
                    wait_for(act, "projected", b, j - 2)
                evacuate(a_T[:, j % 2].rearrange("p h q -> p (h q)"), bank("turn", b, j)[:], "turn", b, j, 0, "attn_T")

            def prep(i):
                act.wait_ge(filled, where["prep", 0, i, 0] + 1)
                copy(xw_T[:, i].rearrange("p k c -> p (k c)"), bank("prep", 0, i, 0)[:].bitcast(BF16)[:, 0:CK * C])\
                    .then_inc(xw_T_done, 1)

            def stack(kind, b, i, dst, slots, name):
                if i >= slots:
                    wait_filled(act, "xscore", b, 2 * (i - slots) + 1, 1)
                else:
                    wait_filled(act, "xscore", b - 1, 2 * (i - slots + QUADS) + 1, 1)
                evacuate(dst[:, i % slots].rearrange("p a q -> p (a q)"), bank(kind, b, i)[:], kind, b, i, 0, name)

            def xexp(b, hp):
                for n in range(4):
                    wait_for(act, "xmasked", b, 3 * (2 * hp + n // 2) + 2)
                    activation(xs[:, hp % 2, n, :], xs[:, hp % 2, n, :], ACT.Exp, bias=xneg[:, hp % 2, n:n + 1])\
                        .then_inc(sig["xexp"], 1)

            def turn_p(b, h):
                if h % 2 == 0:
                    g = h // 4
                    wait_filled(act, "xmix", b if g else b - 1, g - 1 if g else QUADS - 1)
                    evacuate(xp_T[:, (h // 2) % 2, 0].rearrange("p k q -> p (k q)"), bank("turn_p", b, h)[:],
                             "turn_p", b, h, 0, "probs_T_even")

            def route_exp(b):
                wait_for(act, "route", b, 1)
                activation(prob[:], r_in[:], ACT.Exp).then_inc(sig["route_exp"], 1)

            def hidden(b, part):
                wait_filled(act, "ffn", b - 1, 1)
                for n in range(HT // HPARTS // 2):
                    i = part * (HT // HPARTS // 2) + n
                    wait_filled(act, "hidden", b, part, 2 * n)
                    activation(g_T[:, 2 * i:2 * i + 2, :].rearrange("p t n -> p (t n)"),
                               bank("hidden", b, part, 2 * n)[:], ACT.Gelu).then_inc(sig["gelu"], 1)

            for kind, b, i in plan:
                if kind == "split_x":
                    split_x(b)
                elif kind == "piece":
                    split_piece(i)
                elif kind == "val":
                    val(b)
                elif kind in ("near", "far"):
                    score(kind, b, i)
                elif kind == "turn":
                    turn(b, i)
                elif kind == "prep":
                    prep(i)
                elif kind == "turn_k":
                    stack(kind, b, i, kS, QUADS, "k_T")
                elif kind == "turn_q":
                    stack(kind, b, i, qS, 2, "q_T")
                elif kind == "xscore":
                    xexp(b, i)
                elif kind == "turn_p":
                    turn_p(b, i)
                elif kind == "turn_x":
                    evacuate(q_intT[:].rearrange("p k q -> p (k q)"), bank(kind, b)[:].bitcast(BF16)[:, 0:CK * T],
                             kind, b, 0, 0, "y_T")
                elif kind == "turn_ox":
                    evacuate(q_intT[:].rearrange("p k q -> p (k q)"), bank(kind, b)[:].bitcast(BF16)[:, 0:CK * T],
                             kind, b, 0, 0, "o_T")
                elif kind == "xmix":
                    wait_filled(act, "turn_o", b - 1, 1)
                    evacuate(xo_T[:, i, :], bank(kind, b, i)[:, 0:T], kind, b, i, 0, "xout")
                elif kind == "turn_z":
                    wait_filled(act, "hidden", b - 1, HPARTS - 1, HT // HPARTS - 1)
                    evacuate(z_T[:].rearrange("p k q -> p (k q)"), bank(kind, b)[:], kind, b, 0, 0, "z_T")
                elif kind == "route":
                    wait_filled(act, kind, b)
                    activation(lg_T[:], bank(kind, b)[0:NBLK, 0:T], ACT.Identity, bias=br_s[:])\
                        .then_inc(sig["logits"], 1)
                elif kind == "turn_r":
                    route_exp(b)
                elif kind == "turn_m":
                    evacuate(keep_T[:], bank(kind, b)[0:NBLK, :].bitcast(BF16)[:, 0:T], kind, b, 0, 0, "mask_T")
                elif kind == "hidden":
                    hidden(b, i)

        @block.vector
        def _(dve):
            v = nc.vector

            def steps(semaphore, base):
                n = [base]

                def do(ins):
                    ins.then_inc(semaphore, 1)
                    n[0] += 1

                def done():
                    dve.wait_ge(semaphore, n[0])
                return do, done

            def split_piece(n):
                dve.wait_ge(piece_hi, n + 1)
                c = PIECES - 1 if n == 0 else n - 1
                cols = slice(c * PW, (c + 1) * PW)
                v.tensor_tensor(wq_lo[:, :, cols], stage[:, n % 3], wq_hi[:, :, cols].bitcast(F32), ALU.subtract)\
                    .then_inc(piece_lo, 1)

            def split_x(b):
                wait_for(dve, "x_hi", b)
                v.tensor_tensor(x_lo[:], xT_s[:], x_hi[:].bitcast(F32), ALU.subtract).then_inc(sig["x_lo"], 1)

            def rope(b, i):
                ps = bank("rot", b, i)[:].rearrange("p (h q) -> p h q", h=2)
                n = b * (PAIRS + 1) + i
                if n >= 2:
                    dve.wait_ge(sig["rotated"], n - 1)
                if i == 0:
                    wait_filled(dve, "far", b - 1, QUADS - 1)
                    dst = k_T[:]
                else:
                    j = i - 1
                    wait_filled(dve, "far", *((b, (j - 4) // 2) if j >= 4 else (b - 1, (j + PAIRS - 4) // 2)))
                    dst = q_T[:, j % 4]
                wait_filled(dve, "rot", b, i)
                c, s = (a[:].unsqueeze(1).to_broadcast([P, 2, T]) for a in (cos_s, sin_s))
                v.tensor_tensor(dst, ps, c, ALU.mult).then_inc(sig["roped"], 1)
                lower, upper = slice(0, HD // 2), slice(HD // 2, HD)
                t = rope_t[:, n % 2]
                v.tensor_tensor(t[lower], ps[upper], s[upper], ALU.mult).then_inc(sig["roped"], 1)
                v.tensor_tensor(t[upper], ps[lower], s[lower], ALU.mult).then_inc(sig["roped"], 1)

            def mix(b, i):
                j, t = divmod(i, 2)
                wait_filled(dve, "mix", b, i)
                if j < 2:
                    wait_filled(dve, "turn", b - 1, PAIRS - 2 + j)
                else:
                    wait_filled(dve, "turn", b, j - 2)
                ps = bank("mix", b, i)[:, 0:2 * (HD + 1)].rearrange("p (h d) -> p h d", h=2)
                rec = a_rec[:, i % 2, :].unsqueeze(2)
                v.reciprocal(rec, ps[:, :, HD:HD + 1]).then_inc(sig["attn_rec"], 1)
                wait_for(dve, "attn_rec", b, i)
                v.tensor_tensor(a_s[:, j % 2, t], ps[:, :, 0:HD], rec.to_broadcast([P, 2, HD]), ALU.mult)\
                    .then_inc(sig["attn"], 1)

            def layer_norm(n, b, do, done, h, y, tiles=range(TT)):
                done()
                for t in tiles:
                    do(v.bn_stats(stats[n][:, t, :], h[:, t, :]))
                done()
                for t in tiles:
                    do(v.bn_aggr(moments[n][:, t, :], stats[n][:, t, :]))
                done()
                c = slice(tiles[0], tiles[-1] + 1)
                do(v.tensor_scalar(var_eps[n][:, c], moments[n][:, c, 1], EPS_LN, None, ALU.add))
                wait_for(dve, f"rstd{n + 1}", b, 0 if len(tiles) == TT else tiles[0])
                for t in tiles:
                    do(v.tensor_scalar(y[:, t, :], h[:, t, :], moments[n][:, t, 0:1], rstd[n][:, t:t + 1],
                                       ALU.subtract, ALU.mult))

            def norm1(b):
                wait_for(dve, "projected", b, PAIRS - 1)
                dve.wait_ge(xtok_in, 16 * (b + 1))
                do, done = steps(sig["ln1"], b * PER["ln1"])
                do(v.tensor_tensor(x_s[:], acc[:], x_s[:], ALU.add))
                wait_for(dve, "ln2", b - 1, 3)
                layer_norm(0, b, do, done, x_s, y1)

            def quantise(src, do, done):
                do(v.tensor_reduce(q_amax[:], src[:], AX_X, ALU.max, apply_absolute_value=True))
                done()
                do(v.tensor_scalar(q_scale[:], q_amax[:], 1.0 / QMAX, EPS_Q, ALU.mult, ALU.max))
                done()
                do(v.reciprocal(q_rs[:], q_scale[:]))
                done()
                for t in range(TT):
                    do(v.tensor_scalar(q_tmp[:, t, :], src[:, t, :], q_rs[:, t:t + 1], QMAX, ALU.mult, ALU.min))
                done()
                do(v.tensor_scalar(q_tmp[:], q_tmp[:], -QMAX, ROUND, ALU.max, ALU.add))
                done()
                do(v.tensor_scalar(q_int[:], q_tmp[:], ROUND, None, ALU.subtract))

            def prep(i):
                src = (z, y1)[i]
                dve.wait_ge(xw_in, 32)
                do, done = steps(quant_w, 7 * i)
                if i:
                    dve.wait_ge(filled, where["prep", 0, 0, 1] + 1)
                quantise(src, do, done)
                done()
                for o in range(CK):
                    v.tensor_scalar(q_tmp[:, o, 0:P], ident_s[:], q_scale[:, o:o + 1], None, ALU.mult)\
                        .then_inc(scale_diag, 1)
                factor = XD ** -0.5 if i == 0 else 1.0
                dve.wait_ge(filled, where["prep", 0, i, 1] + 1)
                v.tensor_scalar(xw_scale[:, i, :], bank("prep", 0, i, 1)[:, 0:C], factor, None, ALU.mult)\
                    .then_inc(xw_scale_done, 1)
                if i == 0:
                    dve.wait_ge(xbias_in, 16)
                    v.tensor_scalar(bias_s[:, 0, :], bias_s[:, 0, :], factor, None, ALU.mult).then_inc(bias_scaled, 1)

            def context(b, t):
                do, done = steps(sig["kv"], b * PER["kv"] + 4 * t)
                wait_filled(dve, "ctx", b, t)
                if t == 0:
                    wait_for(dve, "ln2", b - 1, 10)
                    wait_filled(dve, "xmix", b - 1, QUADS - 1)
                    wait_filled(dve, "turn_q", b - 1, QUADS - 1)
                    if b == 0:
                        dve.wait_ge(xbias_in, 16)
                        dve.wait_ge(filled, where["prep", 0, 1, 1] + 1)
                ps = bank("ctx", b, t)
                do(v.tensor_tensor(q_tmp[:, t, :], ps[:, 0:C], bias_s[:, 1, :], ALU.add))
                do(v.tensor_tensor(xv_s[:, t, :, 0:XD], ps[:, C:2 * C].rearrange("p (h c) -> p h c", h=XH),
                                   bias_s[:, 2, :].rearrange("p (h c) -> p h c", h=XH), ALU.add))
                done()
                k = q_tmp[:, t, :].rearrange("p (h c) -> p h c", h=XH).unsqueeze(2).to_broadcast([P, XH, 2, XD])
                do(v.tensor_copy(parts[:, t, :, 0:4:2, :], k))
                done()
                do(v.tensor_tensor(parts[:, t, :, 1:4:2, :], k, parts[:, t, :, 0:4:2, :].bitcast(F32), ALU.subtract))

            def quant_x(b):
                wait_filled(dve, "turn_ox", b - 1)
                if b == 0:
                    dve.wait_ge(filled, where["prep", 0, 1, 0] + 1)
                do, done = steps(sig["quant_y"], b * PER["quant_y"])
                wait_for(dve, "ln1", b, 7)
                wait_for(dve, "kv", b, 7)
                quantise(y1, do, done)

            def dequantise(ps, w, do):
                for t in range(TT):
                    do(v.scalar_tensor_tensor(q_tmp[:, t, :], ps[:, t * C:(t + 1) * C], q_scale[:, t:t + 1],
                                              xw_scale[:, w, :], ALU.mult, ALU.mult))

            def query(b):
                wait_filled(dve, "query", b)
                if b == 0:
                    dve.wait_ge(xw_scale_done, 2)
                    dve.wait_ge(bias_scaled, 1)
                do, done = steps(sig["query"], b * PER["query"])
                dequantise(bank("query", b), 0, do)
                done()
                do(v.tensor_tensor(q_tmp[:], q_tmp[:], bias_s[:, 0:1, :].to_broadcast([P, TT, C]), ALU.add))
                done()
                wait_filled(dve, "turn_k", b, QUADS - 1)
                q = q_tmp[:].rearrange("p t (h c) -> p (t h) c", h=XH).unsqueeze(2).to_broadcast([P, TT * XH, 2, XD])
                qp = parts[:].rearrange("p t h l c -> p (t h) l c")
                do(v.tensor_copy(qp[:, :, 0:2, :], q))
                done()
                do(v.tensor_tensor(qp[:, :, 2:4, :], q, qp[:, :, 0:2, :].bitcast(F32), ALU.subtract))

            def xscore(b, hp):
                do, done = steps(sig["xmasked"], b * PER["xmasked"] + 6 * hp)
                if hp == 0:
                    dve.wait_ge(mask_in, 16 * (b + 1))
                s = hp % 2
                for m in range(2):
                    wait_filled(dve, "turn_p", *((b, 2 * (hp - 2) + m) if hp >= 2 else (b - 1, 2 * (hp - 2) + m + XH)))
                    wait_filled(dve, "xscore", b, hp, m)
                    for t in range(TT):
                        n = 2 * m + t
                        do(v.tensor_tensor_reduce(out=xs[:, s, n, :], in0=bank("xscore", b, hp, m)[:, t * T:(t + 1) * T],
                                                  in1=mask_s[:, t, :], scale=1.0, scalar=-3.0e38, op0=ALU.add,
                                                  op1=ALU.max, accum_out=xmax[:, s, n:n + 1]))
                    done()
                    do(v.tensor_scalar(xneg[:, s, 2 * m:2 * m + 2], xmax[:, s, 2 * m:2 * m + 2], -1.0, None, ALU.mult))

            def turn_p(b, h):
                if h % 2:
                    g = h // 4
                    wait_filled(dve, "xmix", b if g else b - 1, g - 1 if g else QUADS - 1)
                    wait_filled(dve, "turn_p", b, h)
                    v.tensor_copy(xp_T[:, (h // 2) % 2, 1].rearrange("p k q -> p (k q)"), bank("turn_p", b, h)[:])\
                        .then_inc(sig["probs_T_odd"], 1)

            def turn_o(b, t):
                wait_filled(dve, "turn_o", b, t)
                ps = bank("turn_o", b, t)[:].rearrange("p (h w) -> p h w", w=XW)
                rec = xrec[:, t, :].unsqueeze(2)
                v.reciprocal(rec, ps[:, :, XD:XD + 1]).then_inc(sig["xattn"], 1)
                wait_for(dve, "xattn", b, 2 * t)
                v.tensor_tensor(q_tmp[:, t, :].rearrange("p (h c) -> p h c", h=XH), ps[:, :, 0:XD],
                                rec.to_broadcast([P, XH, XD]), ALU.mult).then_inc(sig["xattn"], 1)

            def quant_o(b):
                do, done = steps(sig["quant_o"], b * PER["quant_o"])
                wait_for(dve, "xattn", b, 2 * TT - 1)
                wait_for(dve, "query", b, 4)
                quantise(q_tmp, do, done)

            def outproj(b):
                wait_filled(dve, "outproj", b)
                do, done = steps(sig["ln2"], b * PER["ln2"])
                dequantise(bank("outproj", b), 1, do)
                done()
                do(v.tensor_tensor(q_tmp[:], q_tmp[:], bias_s[:, 3:4, :].to_broadcast([P, TT, C]), ALU.add))
                done()
                do(v.tensor_tensor(q_tmp[:], q_tmp[:], y1[:], ALU.add))
                wait_filled(dve, "turn_z", b - 1)
                wait_for(dve, "ln3", b - 1, 5)
                layer_norm(1, b, do, done, q_tmp, z)

            def router(b):
                do, done = steps(sig["route"], b * PER["route"])
                wait_filled(dve, "turn_r", b)
                ps = bank("turn_r", b)[:, 0:TT * NBLK].rearrange("p (t n) -> p t n", t=TT)
                wide = lambda a: a[:].unsqueeze(2).to_broadcast([P, TT, NBLK])
                do(v.tensor_reduce(r_max[:], ps, AX_X, ALU.max))
                done()
                do(v.tensor_tensor(r_in[:], ps, wide(r_max), ALU.subtract))
                wait_for(dve, "route_exp", b)
                do(v.tensor_reduce(r_sum[:], prob[:], AX_X, ALU.add))
                done()
                do(v.reciprocal(r_rec[:], r_sum[:]))
                done()
                do(v.tensor_tensor(prob[:], prob[:], wide(r_rec), ALU.mult))
                done()
                other = prob[:].unsqueeze(2).to_broadcast([P, TT, NBLK, NBLK])
                own = prob[:].unsqueeze(3).to_broadcast([P, TT, NBLK, NBLK])
                do(v.tensor_tensor(above[:], other, own, ALU.is_gt))
                do(v.tensor_tensor(equal[:], other, own, ALU.is_equal))
                done()
                if b == 0:
                    dve.wait_ge(consts_set, CONSTS)
                do(v.tensor_tensor(equal[:], equal[:], before_s[:].unsqueeze(1).to_broadcast([P, TT, NBLK, NBLK]),
                                   ALU.mult))
                done()
                do(v.tensor_tensor(above[:], above[:], equal[:], ALU.add))
                done()
                do(v.tensor_reduce(rank[:], above[:], AX_X, ALU.add))
                done()
                wait_filled(dve, "turn_m", b - 1)
                do(v.tensor_scalar(keep[:], rank[:], TOPK - 0.5, None, ALU.is_lt))

            def hidden(b, part):
                for n in range(HT // HPARTS // 2):
                    i = part * (HT // HPARTS // 2) + n
                    g = g_T[:, 2 * i:2 * i + 2, :].rearrange("p t n -> p (t n)")
                    wait_for(dve, "gelu", b, i)
                    wait_filled(dve, "hidden", b, part, 2 * n + 1)
                    v.tensor_tensor(g, g, bank("hidden", b, part, 2 * n + 1)[:], ALU.mult).then_inc(sig["masked"], 1)

            def ffn(b, t):
                wait_filled(dve, "ffn", b, t)
                do, done = steps(sig["ln3"], b * PER["ln3"] + 5 * t)
                do(v.tensor_tensor(h3[:, t, :], bank("ffn", b, t)[:, 0:C], z[:, t, :], ALU.add))
                if b and t == 0:
                    dve.wait_ge(sig["stored"], 16 * TT * b)
                layer_norm(2, b, do, done, h3, y3, [t])

            dve.wait_ge(tables_in, 48)
            for kind, b, i in plan:
                if kind == "split_x":
                    split_x(b)
                elif kind == "piece":
                    split_piece(i)
                elif kind == "rot":
                    rope(b, i)
                elif kind == "mix":
                    mix(b, i)
                elif kind == "norm1":
                    norm1(b)
                elif kind == "prep":
                    prep(i)
                elif kind == "ctx":
                    context(b, i)
                elif kind == "quant_x":
                    quant_x(b)
                elif kind == "query":
                    query(b)
                elif kind == "xscore":
                    xscore(b, i)
                elif kind == "turn_p":
                    turn_p(b, i)
                elif kind == "turn_o":
                    turn_o(b, i)
                elif kind == "quant_o":
                    quant_o(b)
                elif kind == "outproj":
                    outproj(b)
                elif kind == "turn_r":
                    router(b)
                elif kind == "hidden":
                    hidden(b, i)
                elif kind == "ffn":
                    ffn(b, i)

        @block.gpsimd
        def _(pool):
            g = nc.gpsimd

            def constants():
                def select(out, pattern, base, channel, op):
                    g.affine_select(out=out, in_=out, compare_op=op, fill=0.0, base=base, pattern=pattern,
                                    channel_multiplier=channel).then_inc(consts_set, 1)

                g.memset(ones[:], 1.0).then_inc(consts_set, 1)
                g.memset(half[:], -0.5).then_inc(consts_set, 1)
                g.memset(v_s[:, :, :, HD:HD + 1], 1.0).then_inc(consts_set, 1)
                g.memset(xv_s[:, :, :, XD:XD + 1], 1.0).then_inc(consts_set, 1)
                g.memset(xv_s[:, :, :, XD + 1:XW], 0.0).then_inc(consts_set, 1)
                g.memset(identb_s[:], 1.0).then_inc(consts_set, 1)
                g.memset(pick_s[:], 1.0).then_inc(consts_set, 1)
                g.memset(before_s[:], 1.0).then_inc(consts_set, 1)
                pool.wait_ge(consts_set, 8)
                select(identb_s[:], [[-1, P]], 0, 1, ALU.is_equal)
                select(before_s[:], [[1, NBLK], [-1, NBLK]], 0, 0, ALU.is_gt)
                select(pick_s[:], [[P, HT], [1, P]], 0, -BLK, ALU.is_ge)
                pool.wait_ge(consts_set, 11)
                select(pick_s[:], [[-P, HT], [-1, P]], BLK - 1, BLK, ALU.is_ge)

            def rotate(b, i):
                n = b * (PAIRS + 1) + i
                dst = k_T[:] if i == 0 else q_T[:, (i - 1) % 4]
                wait_for(pool, "roped", b, 3 * i + 2)
                g.tensor_tensor(dst, dst, rope_t[:, n % 2], ALU.add).then_inc(sig["rotated"], 1)

            def causal(kind, b, i):
                wait_for(pool, "expd", b, tile_at[kind, i])
                p, heads = (p_near[:, i % NEAR, :, 0:P], 2) if kind == "near" else (p_far[:, i % 2], 4)
                g.affine_select(out=p, in_=p, compare_op=ALU.is_ge, fill=0.0, base=0,
                                pattern=[[0, heads], [1, P]], channel_multiplier=-1).then_inc(sig["causal"], 1)

            def inverse_root(n, b, name, step, c=slice(0, TT)):
                wait_for(pool, name, b, step)
                g.tensor_tensor(rstd[n][:, c], var_eps[n][:, c], half[:, c], ALU.pow).then_inc(sig[f"rstd{n + 1}"], 1)

            constants()
            pool.wait_ge(consts_set, CONSTS)
            for kind, b, i in plan:
                if kind == "rot":
                    rotate(b, i)
                elif kind in ("near", "far"):
                    causal(kind, b, i)
                elif kind == "norm1":
                    inverse_root(0, b, "ln1", 5)
                elif kind == "outproj":
                    inverse_root(1, b, "ln2", 8)
                elif kind == "ffn":
                    inverse_root(2, b, "ln3", 5 * i + 3, slice(i, i + 1))


def rope_tables():
    freq = (np.float32(1.0) / np.float32(10000.0) ** (np.arange(0, HD, 2, dtype=np.float32) / np.float32(HD)))
    angle = np.outer(freq.astype(np.float32), np.arange(T, dtype=np.float32)).astype(np.float32)
    cos, sin = np.cos(angle), np.sin(angle)
    return np.concatenate([cos, cos]), np.concatenate([sin, -sin])


def kernel(**inputs):
    import concourse.bacc as bacc
    from concourse.bass_utils import run_bass_kernel_spmd

    a = {k: np.asarray(v) for k, v in inputs.items()}
    cos, sin = rope_tables()
    arrays = {
        "x": a["x"],
        "xT": a["x"].transpose(0, 2, 1),
        "ctxT": a["ctx_2048"].transpose(0, 2, 1),
        "mask": a["mask_BxSxS2_ff0"],
        "wqkv": a["L0_attn_Wqkv"],
        "wo": a["L0_attn_Wo"],
        "wkvT": np.concatenate([a["L0_xattn_wk"].T, a["L0_xattn_wv"].T], 1),
        "xwq": a["L0_xattn_wq"],
        "xwo": a["L0_xattn_wo"],
        "xbias": np.concatenate([a[f"L0_xattn_b{n}"] for n in "qkvo"]),
        "wrT": a["L0_ffn_Wr"].T,
        "br": a["L0_ffn_br"].reshape(NBLK, 1),
        "w1T": a["L0_ffn_W1"].T,
        "w2T": a["L0_ffn_W2"].T,
        "cos": cos,
        "sin": sin,
        "ident": np.eye(P, dtype=np.float32),
    }
    arrays = {f"in_{k}": np.ascontiguousarray(v) for k, v in arrays.items()}
    nc = bacc.Bacc("TRN2", target_bir_lowering=False, num_devices=1)
    args = [nc.dram_tensor(k, v.shape, mybir.dt.from_np(v.dtype), kind="ExternalInput").ap() for k, v in arrays.items()]
    out = nc.dram_tensor("out_y", (B, T, C), F32, kind="ExternalOutput").ap()
    build_decoder(nc, *args, out)
    r = run_bass_kernel_spmd(nc, [arrays], core_ids=[0])
    return r.results[0]["out_y"]
```

```python
from contextlib import ExitStack

import numpy as np

import concourse.bass as bass
from concourse import mybir

F32 = mybir.dt.float32
F32R = mybir.dt.float32r
BF16 = mybir.dt.bfloat16
ACT = mybir.ActivationFunctionType
ALU = mybir.AluOpType
AX_X = mybir.AxisListType.X

P = 128
B, T, C = 4, 256, 256
TT = T // P
CK = C // P
NH, NKV, HD = 16, 2, 128
PAIRS = NH // 2
PAIR = 2 * HD
QUADS = NH // 4
SCALE = 0.08838834764831845
SOFTCAP = 30.0
XH, XD = 16, C // 16
XPAIRS = XH // 2
XW = 2 * XD
NBLK, BLK, TOPK = 16, 64, 4
HID = NBLK * BLK
HT = HID // P
EPS_LN, EPS_Q, QMAX = 1e-5, 1e-8, 127.0
ROUND = 12582912.0
NBANK = 7
NEAR = 3
CONSTS = 12
HPARTS = 2
PIECES = 5
PW = (NH + 2 * NKV) * HD // PIECES



def rotate_ops(b):
    ops = [("split_x", 0)]
    if b == 0:
        ops += [("piece", 0), ("piece", 1)]
    for i in range(PAIRS + 1):
        ops.append(("rot", i))
        if b == 0 and i % 2 and i < PAIRS - 1:
            ops.append(("piece", (i + 3) // 2))
    return [(kind, b, i, 0) for kind, i in ops]


def score_ops(b):
    ops = []
    for j in range(PAIRS):
        ops += [("near", j)] + [("far", j // 2)] * (j % 2)
    return [(kind, b, i, 0) for kind, i in ops]


def mix_ops(b):
    ops = [("val", 0)]
    for j in range(PAIRS + 2):
        if j < PAIRS:
            ops += [("mix", 2 * j), ("mix", 2 * j + 1)]
        if 0 <= j - 1 < PAIRS:
            ops.append(("turn", j - 1))
        if 0 <= j - 2 < PAIRS:
            ops.append(("proj", j - 2))
    return [(kind, b, i, 0) for kind, i in ops] + [("norm1", b, 0, t) for t in range(TT)]


def context_ops(b):
    prep = [(kind, 0, i, 0) for i in range(2) for kind in ("quant_w", "turn_w")] if b == 0 else []
    return [*prep, *(("ctx", b, t, 0) for t in range(TT)), *(("turn_k", b, g, 0) for g in range(QUADS))]


def cross_ops(b, t):
    ops = [("quant_x", 0), ("turn_x", 0), ("query", 0), ("turn_q", 0), ("xscore", 0), ("turn_q", 1)]
    for g in range(QUADS):
        ops += [("turn_p", 2 * g), ("turn_p", 2 * g + 1)]
        if g + 1 < QUADS:
            ops.append(("xscore", g + 1))
        if g + 2 < QUADS:
            ops.append(("turn_q", g + 2))
        ops.append(("xmix", g))
    ops += [("turn_o", 0), ("quant_o", 0), ("turn_ox", 0), ("outproj", 0)]
    return [(kind, b, i, t) for kind, i in ops]


def network_ops(b, t):
    ops = [("turn_z", 0), ("route", 0), ("turn_r", 0), ("turn_m", 0), *(("hidden", i) for i in range(HPARTS)), ("ffn", 0)]
    return [(kind, b, i, t) for kind, i in ops]


BANKS = {"rot": 1, "val": 1, "near": 1, "far": 1, "mix": 1, "turn": 1, "ctx": 1, "turn_x": 1, "query": 1,
         "turn_k": 1, "turn_q": 1, "xscore": 2, "turn_p": 1, "xmix": 1, "turn_o": 1, "turn_ox": 1,
         "outproj": 1, "turn_z": 1, "route": 1, "turn_r": 1, "turn_m": 1, "hidden": 2, "ffn": 1, "turn_w": 2}
STAGES = {
    "split_x": "A500 D600", "piece": "A900 D1100", "quant_w": "D2900", "turn_w": "P650 D350",
    "rot": "P1310 D1860 G1250", "val": "P1310 A500",
    "near": "P870 A1130 G400", "far": "P870 A1130 G600", "mix": "P650 D550", "turn": "P430 A480",
    "proj": "P1750", "norm1": "D1100 G460 D350", "ctx": "P1730 D2150", "turn_k": "P430 A480", "quant_x": "D1700 G1100",
    "turn_x": "P110 A260", "query": "P220 D2050", "turn_q": "P220 A270", "xscore": "P430 D1400 a1650",
    "turn_p": "P430 A480", "turn_p_odd": "P430 D600", "xmix": "P530 A170", "turn_o": "P430 D650",
    "quant_o": "D1700", "turn_ox": "P110 A260",
    "outproj": "P220 D1650 G460 D350", "turn_z": "P220 A270", "route": "P440 A260", "turn_r": "P60 D320 A100 D2650",
    "turn_m": "P60 A130", "hidden": "P2000 A480 D600", "ffn": "P3500 D1100 G460 D350"}
TABLES = {"near": "exp", "far": "exp", "xscore": "exp", "turn_r": "exp", "hidden": "gelu"}
TABLE_LOAD = 1280
HOP = 200
PHASES = 4
ARRIVAL = {"split_x": lambda i: 3500, "piece": lambda i: 5000 + 2900 * i, "quant_w": lambda i: 30000, "ctx": lambda i: 35000,
           "proj": lambda i: 28000, "hidden": lambda i: 50000}
CREDIT = {
    "context": [1000, 1000, 200, 1000, 1000, 600, 800, 500, 500, 800, 1000, 1000, -3000, -3000, -900, 1000],
    "cross0": [1000, 1000, 1000, 1000, 1000, 1000, 900, 1000, 900, 1000, 700, -3100, -10900, -10800, -18100, -17100],
    "cross1": [900, 1000, 1000, 1000, 1000, 1000, 1000, 1000, 1000, 600, -2700, -3100, -10600, -11000, -18300, -17100],
    "network0": [1000, 700, 1000, 100, -2600, -2500, -12900, -11800, -10500, -16700, -18400, -20900, -1600, -17700, -25400, -33200],
    "network1": [700, 600, 1000, -200, -3100, -3100, -9100, -12800, -10100, -18600, -6900, -18700, -15500, -16000, -18600, -34700],
    "rotate": [1000, 900, -200, 300, 1000, 1000, 1000, 1000, 1000, 1000, 800, 800, 1000, 500, 600, 400],
    "score": [1000, -100, 1000, 1000, 1000, 1000, 1000, 1000, 900, 1000, 700, 1000, 0, 700, 900, -3200],
    "mix": [-200, 1000, 900, 1000, 1000, 600, 900, 1000, 900, 300, 800, 1000, 1000, 300, -3300, -3100]}


def sources(op):
    kind, b, i, t = op
    past = lambda kind, b, i, n: (kind, b, i, 0) if i >= 0 else (kind, b - 1, i + n, 0)
    both = lambda kind, b: [(kind, b, 0, n) for n in range(TT)]
    table = {
        "split_x": [("rot", b - 1, PAIRS, 0), ("val", b - 1, 0, 0)],
        "quant_w": [("turn_w", 0, i - 1, 0)],
        "turn_w": [("quant_w", 0, i, 0)],
        "rot": [("split_x", b, 0, 0), ("piece", 0, 1 + (i - 1) // 2 if i else 0, 0), past("far", b, (i - 5) // 2 if i else -1, QUADS)],
        "near": [("rot", b, i + 1, 0), past("mix", b, 2 * (i - NEAR) + 1, NH) if i >= NEAR else
                 ("mix", b - 1, 2 * range(i, PAIRS, NEAR)[-1] + 1, 0)],
        "far": [("rot", b, 2 * i + 2, 0), past("mix", b, 4 * (i - 2) + 3, NH)],
        "val": [("split_x", b, 0, 0), ("mix", b - 1, NH - 1, 0), ("piece", 0, 0, 0)],
        "mix": [("val", b, 0, 0), ("near", b, i // 2, 0)] + [("far", b, i // 4, 0)] * (i % 2) + [past("turn", b, i // 2 - 2, PAIRS)],
        "turn": [("mix", b, 2 * i + 1, 0), past("proj", b, i - 2, PAIRS)],
        "proj": [("turn", b, i, 0)] + both("norm1", b - 1) * (i == 0),
        "norm1": [("proj", b, PAIRS - 1, 0), *both("outproj", b - 2)],
        "ctx": [("xmix", b - 1, QUADS - 1, n) for n in range(TT)],
        "turn_k": [("ctx", b, 1, 0), *(("xscore", b - 1, i, n) for n in range(TT))],
        "quant_x": [("norm1", b, 0, t), ("turn_w", 0, 1, 0)],
        "turn_x": [("quant_x", b, 0, t)],
        "query": [("turn_x", b, 0, t), ("turn_k", b, QUADS - 1, 0)],
        "turn_q": [("query", b, 0, t), ("xscore", b, i - 2, t)],
        "xscore": [("turn_q", b, i, t), ("turn_k", b, i, 0)],
        "turn_p": [("xscore", b, i // 2, t)],
        "xmix": [("turn_p", b, 2 * i, t), ("turn_p", b, 2 * i + 1, t)],
        "turn_o": [("xmix", b, QUADS - 1, t)],
        "quant_o": [("turn_o", b, 0, t)],
        "turn_ox": [("quant_o", b, 0, t)],
        "outproj": [("turn_ox", b, 0, t), ("ffn", b - 2, 0, t)],
        "turn_z": [("outproj", b, 0, t)],
        "route": [("turn_z", b, 0, t)],
        "turn_r": [("route", b, 0, t)],
        "turn_m": [("turn_r", b, 0, t)],
        "hidden": [("turn_m", b, 0, t)],
        "ffn": [("hidden", b, n, t) for n in range(HPARTS)],
    }
    return [s for s in table.get(kind, []) if s[1] >= 0 and s[2] >= 0]


def make_plan():
    every = range(B)
    streams = [("context", [op for b in every for op in context_ops(b)]),
               *((f"cross{t}", [op for b in every for op in cross_ops(b, t)]) for t in range(TT)),
               *((f"network{t}", [op for b in every for op in network_ops(b, t)]) for t in range(TT)),
               ("mix", [op for b in every for op in mix_ops(b)]),
               ("score", [op for b in every for op in score_ops(b)]),
               ("rotate", [op for b in every for op in rotate_ops(b)])]
    free = dict.fromkeys("PADG", 0)
    free["table"] = "exp"
    needs = {op: sources(op) for _, ops in streams for op in ops}
    stages = {kind: [(s[0], int(s[1:])) for s in text.split()] for kind, text in STAGES.items()}
    kind = lambda op: "turn_p_odd" if op[0] == "turn_p" and op[2] % 2 else op[0]
    phase = {}
    for _, ops in streams:
        for b in every:
            own = [op for op in ops if op[1] == b]
            phase |= {op: b * PHASES + n * PHASES // len(own) for n, op in enumerate(own)}
    end, released, plan = {}, [], []

    def run(op):
        now = max([end[s] + HOP for s in needs[op]] + [ARRIVAL[op[0]](op[2]) if op[0] in ARRIVAL and op[1] == 0 else 0])
        after, start, release = dict(free), None, None
        for engine, length in stages[kind(op)]:
            if engine == "a":
                engine, now = "A", now - last // 2
            if engine == "P" and op[0] in BANKS and len(released) >= NBANK:
                now = max(now, released[BANKS[op[0]] - NBANK - 1] + HOP)
            now = max(now, after[engine])
            start = now if start is None else start
            if engine == "A" and TABLES.get(op[0], after["table"]) != after["table"]:
                after["table"] = TABLES[op[0]]
                now += TABLE_LOAD
            now += length
            after[engine], last = now, length
            if engine != "P" and release is None:
                release = now
            now += HOP
        return start, now - HOP, after, release

    while any(ops for _, ops in streams):
        ready = []
        for rank, (name, ops) in enumerate(streams):
            if ops and all(s in end for s in needs[ops[0]]):
                ready.append((run(ops[0])[0] - CREDIT[name][phase[ops[0]]], rank))
        _, rank = min(ready)
        op = streams[rank][1].pop(0)
        _, end[op], free, release = run(op)
        released += [release] * BANKS.get(op[0], 0)
        plan.append(op)
    return plan


PER = {"x_hi": 1, "x_lo": 1, "roped": 3 * (PAIRS + 1), "rotated": PAIRS + 1, "values": 1,
       "capped": PAIRS + QUADS, "expd": PAIRS + QUADS, "causal": PAIRS + QUADS, "attn_rec": NH,
       "attn": NH, "attn_T": PAIRS, "projected": PAIRS, "kv": 8, "k_T": QUADS}
PER_TILE = {"ln1": 5, "rstd1": 1, "ln2": 6, "ln3": 5, "rstd2": 1, "rstd3": 1, "y1_bias": 1, "mask_neg": 1, "quant_y": 6, "quant_o": 6, "y_T": 1,
            "query": 4, "q_T": QUADS, "xmasked": 4 * QUADS, "xexp": 4 * QUADS, "probs_T_even": QUADS,
            "probs_T_odd": QUADS, "xout": QUADS, "xattn": 2, "o_T": 1, "z_T": 1, "logits": 1, "route": 11,
            "route_exp": 1, "mask_T": 1, "gelu": HPARTS, "masked": HPARTS, "stored": 16}


def build_decoder(nc, x, xT, ctxT, mask, wqkv, wo, wkvT, xwq, xwo, xbias, wrT, br, w1T, w2T,
                  cos, sin, ident, out):
    plan = make_plan()
    where = {}
    n_uses = 0
    for kind, b, i, t in plan:
        for k in range(BANKS.get(kind, 0)):
            where[kind, b, i, t, k] = n_uses
            n_uses += 1
    used = sorted(where, key=where.get)

    with ExitStack() as ctx:
        def sb(name, shape, dt=F32, parts=P):
            return ctx.enter_context(nc.sbuf_tensor(name, [parts, *shape], dt))

        def sem(name):
            return ctx.enter_context(nc.semaphore(name))

        banks = [ctx.enter_context(nc.psum_tensor(f"bank{i}", [P, 512], F32)) for i in range(NBANK)]
        acc = ctx.enter_context(nc.psum_tensor("acc", [P, TT, C], F32))

        stage = sb("stage", [3, CK, PW])
        wq_hi = sb("wqkv_hi", [CK, PIECES * PW], F32R)
        wq_lo = sb("wqkv_lo", [CK, PIECES * PW], F32R)
        wo_s = sb("wo_s", [NH, C])
        wkv_s = sb("wkv_s", [CK, 2 * C])
        w1_s = sb("w1_s", [CK, HID])
        w2_s = sb("w2_s", [HT, C])
        wr_s = sb("wr_s", [CK, NBLK])
        br_s = sb("br_s", [1], parts=NBLK)
        xw_T = sb("xw_T", [2, CK, C], BF16)
        xw_scale = sb("xw_scale", [2, C])
        bias_s = sb("bias_s", [4, C])
        cos_s, sin_s = sb("cos_s", [T]), sb("sin_s", [T])
        ident_s = sb("ident_s", [P])
        identb_s = sb("identb_s", [P], BF16)
        ones = sb("ones", [P])
        pick_s = sb("pick_s", [HT, P], BF16, parts=NBLK)
        before_s = sb("before_s", [NBLK, NBLK], BF16)
        half = sb("half", [TT])

        xT_s = sb("xT_s", [CK, T])
        x_hi, x_lo = sb("x_hi", [CK, T], F32R), sb("x_lo", [CK, T], F32R)
        rope_t = sb("rope_t", [2, 2, T])
        q_T = sb("q_T", [4, 2, T])
        k_T = sb("k_T", [NKV, T])
        v_s = sb("v_s", [TT, NKV, HD + 1])
        p_near = sb("p_near", [NEAR, 2, T])
        p_far = sb("p_far", [2, 4, P])
        a_rec = sb("a_rec", [2, 2])
        a_s = sb("a_s", [2, TT, 2, HD])
        a_T = sb("a_T", [2, 2, T])
        y1 = sb("y1", [2, TT, C])

        ctx_s = sb("ctx_s", [CK, T])
        mask_s = sb("mask_s", [TT, T])
        parts = sb("parts", [TT, XH, 4, XD], F32R)
        kS = sb("kS", [QUADS, 2, T], F32R)
        qS = sb("qS", [TT, 2, 2, P], F32R)
        xv_s = sb("xv_s", [TT, XH, XW])
        xs = sb("xs", [TT, 2, 2, T])
        xneg = sb("xneg", [TT, 2, 2])
        xp_T = sb("xp_T", [TT, 2, 2, TT, P])
        xo_T = sb("xo_T", [TT, QUADS, P])
        xrec = sb("xrec", [2, XH])
        q_tmp = sb("q_tmp", [TT, C])
        q_int = sb("q_int", [TT, C], BF16)
        q_intT = sb("q_intT", [TT, CK, P], BF16)
        q_amax, q_scale, q_rs = sb("q_amax", [TT]), sb("q_scale", [TT]), sb("q_rs", [TT])

        z_T = sb("z_T", [TT, CK, P])
        lg_T = sb("lg_T", [T], parts=NBLK)
        r_max, r_sum, r_rec = sb("r_max", [TT]), sb("r_sum", [TT]), sb("r_rec", [TT])
        r_in, prob = sb("r_in", [TT, NBLK]), sb("prob", [TT, NBLK])
        above = sb("above", [TT, NBLK, NBLK], BF16)
        equal = sb("equal", [TT, NBLK, NBLK], BF16)
        rank = sb("rank", [TT, NBLK])
        keep = sb("keep", [TT, NBLK], BF16)
        keep_T = sb("keep_T", [T], BF16, parts=NBLK)
        flat = stage[:].rearrange("p a c n -> p (a c n)")
        g_T = flat[:, 0:HT * T].rearrange("p (t h n) -> p t h n", t=TT, h=HT)
        z1, y3 = (flat[:, (HT + CK * n) * T:(HT + CK * (n + 1)) * T].rearrange("p (t c) -> p t c", t=TT)
                  for n in range(2))
        z = [sb("z", [TT, C])[:], z1]

        stats = [sb(f"stats{n}", [TT, 6]) for n in (1, 2, 3)]
        moments = [sb(f"moments{n}", [TT, 2]) for n in (1, 2, 3)]
        var_eps = [sb(f"var_eps{n}", [TT]) for n in (1, 2, 3)]
        rstd = [sb(f"rstd{n}", [TT]) for n in (1, 2, 3)]

        sig = {(name, 0): sem(name) for name in PER}
        sig |= {(name, t): sem(f"{name}_tile{t}") for name in PER_TILE for t in range(TT)}
        filled = sem("filled")
        x_in, ctx_in, mask_in = sem("x_in"), sem("ctx_in"), sem("mask_in")
        xtok_in = [sem(f"xtok_in{i}") for i in range(2)]
        piece_in = [sem(f"piece_in{i}") for i in range(PIECES)]
        tables_in, wkv_in, xw_in, xbias_in = sem("tables_in"), sem("wkv_in"), sem("xw_in"), sem("xbias_in")
        wo_in, ffn_in, route_in = sem("wo_in"), sem("ffn_in"), sem("route_in")
        piece_hi, piece_lo = sem("piece_hi"), sem("piece_lo")
        consts_set, bias_scaled = sem("consts_set"), sem("bias_scaled")
        quant_w, scale_diag, xw_T_done, xw_scale_done = (sem("quant_w"), sem("scale_diag"),
                                                         sem("xw_T_done"), sem("xw_scale_done"))

        def count(name, b, i=0):
            return b * (PER | PER_TILE)[name] + i + 1

        def wait_for(eng, name, b, i=0, t=0):
            if b >= 0:
                eng.wait_ge(sig[name, t], count(name, b, i))

        def bank(kind, b, i=0, t=0, k=0):
            return banks[where[kind, b, i, t, k] % NBANK]

        def wait_filled(eng, kind, b, i=0, t=0, k=0):
            if b >= 0:
                eng.wait_ge(filled, where[kind, b, i, t, k] + 1)

        tiles = [(k, i) for k, _, i, _ in score_ops(0)]
        tile_at = {t: n for n, t in enumerate(tiles)}

        def released(key):
            kind, b, i, t, k = key
            table = {
                "rot": ("roped", 3 * i + 2), "val": ("values", 0),
                "near": ("capped", tile_at.get(("near", i))), "far": ("capped", tile_at.get(("far", i))),
                "mix": ("attn", i), "turn": ("attn_T", i), "ctx": ("kv", 4 * i + 1), "turn_x": ("y_T", 0),
                "query": ("query", 0), "turn_k": ("k_T", i), "turn_q": ("q_T", i),
                "xscore": ("xmasked", 4 * i + 2 * k + 1),
                "turn_p": ("probs_T_odd" if i % 2 else "probs_T_even", i // 2), "xmix": ("xout", i),
                "turn_o": ("xattn", 1), "turn_ox": ("o_T", 0), "outproj": ("ln2", 0),
                "turn_z": ("z_T", 0), "route": ("logits", 0), "turn_r": ("route", 1), "turn_m": ("mask_T", 0),
                "hidden": ("gelu" if k == 0 else "masked", i), "ffn": ("ln3", 0),
            }
            if kind == "turn_w":
                return (xw_T_done if k == 0 else xw_scale_done), i + 1
            name, n = table[kind]
            return sig[name, t], count(name, b, n)

        block = ctx.enter_context(nc.Block())

        @block.sync
        def _(sp):
            rows = lambda a: a.rearrange("(k p) n -> p k n", p=P)
            order = [PIECES - 1, *range(PIECES - 1)]

            def load_tokens(b):
                if b == 1:
                    sp.wait_ge(quant_w, 14)
                for t in range(TT):
                    wait_for(sp, "ln2", b - 2, 1, t)
                sp.dma_start(y1[:, b % 2], rows(x[b])).then_inc(xtok_in[b % 2], 16)

            def load_context(b):
                wait_filled(sp, "ctx", b - 1, 1)
                sp.dma_start(ctx_s[:], rows(ctxT[b])).then_inc(ctx_in, 16)

            def load_mask(b):
                for t in range(TT):
                    wait_for(sp, "xmasked", b - 1, 4 * QUADS - 1, t)
                sp.dma_start(mask_s[:], rows(mask[b])).then_inc(mask_in, 16)

            sp.dma_start(xT_s[:], rows(xT[0])).then_inc(x_in, 16)
            sp.dma_start(stage[:, 0], rows(wqkv[:, order[0] * PW:(order[0] + 1) * PW])).then_inc(piece_in[0], 16)
            sp.dma_start(cos_s[:], cos).then_inc(tables_in, 16)
            sp.dma_start(sin_s[:], sin).then_inc(tables_in, 16)
            sp.dma_start(ident_s[:], ident).then_inc(tables_in, 16)
            for n, c in enumerate(order[1:], start=1):
                if n >= 3:
                    sp.wait_ge(piece_lo, 2 * (n - 2))
                sp.dma_start(stage[:, n % 3], rows(wqkv[:, c * PW:(c + 1) * PW])).then_inc(piece_in[n], 16)
            sp.dma_start(wo_s[:], rows(wo)).then_inc(wo_in, 16)
            load_tokens(0)
            for w, a in enumerate((xwq, xwo)):
                sp.dma_start((z[0], y1[:, 1])[w], rows(a)).then_inc(xw_in, 16)
            sp.dma_start(bias_s[:].rearrange("p a c -> p (a c)"), xbias.partition_broadcast(P)).then_inc(xbias_in, 16)
            sp.dma_start(wkv_s[:], rows(wkvT)).then_inc(wkv_in, 16)
            load_context(0)
            load_mask(0)
            sp.dma_start(w1_s[:], rows(w1T)).then_inc(ffn_in, 16)
            sp.dma_start(w2_s[:], rows(w2T)).then_inc(ffn_in, 16)
            sp.dma_start(wr_s[:], rows(wrT)).then_inc(route_in, 16)
            sp.dma_start(br_s[:], br).then_inc(route_in, 16)
            done = set()
            for kind, b, i, t in plan:
                done.add((kind, b, i, t))
                both = all((kind, b, i, n) in done for n in range(TT))
                if kind == "quant_w" and i == 1:
                    load_tokens(1)
                elif kind == "outproj" and both and b + 2 < B:
                    load_tokens(b + 2)
                elif kind == "ctx" and i == TT - 1 and b + 1 < B:
                    load_context(b + 1)
                elif kind == "xscore" and i == QUADS - 1 and both and b + 1 < B:
                    load_mask(b + 1)
                elif kind == "ffn":
                    wait_for(sp, "ln3", b, 4, t)
                    sp.dma_start(out[b, t * P:(t + 1) * P, :], y3[:, t, :]).then_inc(sig["stored", t], 16)
            for t in range(TT):
                sp.wait_ge(sig["stored", t], 16 * B)

        @block.tensor
        def _(pe):
            mm, transpose = nc.tensor.matmul, nc.tensor.transpose

            def claim(kind, b, i=0, t=0, k=0):
                n = where[kind, b, i, t, k]
                if n >= NBANK:
                    pe.wait_ge(*released(used[n - NBANK]))
                return banks[n % NBANK]

            def three_pass(ps, lhs, rhs, k, last):
                for n, (i, j) in enumerate(((0, 0), (0, 1), (1, 0))):
                    ins = mm(ps, lhs[i], rhs[j], start=(k == 0 and n == 0), stop=(last and n == 2))
                return ins

            def rot(b, i):
                ps = claim("rot", b, i)
                wait_for(pe, "x_lo", b)
                pe.wait_ge(piece_lo, 1 if i == 0 else i + 2)
                for m in range(2):
                    c0 = (NH + m if i == 0 else 2 * i - 2 + m) * HD
                    for k in range(CK):
                        w = [a[:, k, c0:c0 + HD] for a in (wq_hi, wq_lo)]
                        ins = three_pass(ps[:, m * T:(m + 1) * T], w, [x_hi[:, k, :], x_lo[:, k, :]], k, k == CK - 1)
                ins.then_inc(filled, 1)

            def val(b):
                ps = claim("val", b)
                wait_for(pe, "x_lo", b)
                pe.wait_ge(piece_lo, 2)
                c0 = (NH + NKV) * HD
                for t in range(TT):
                    for k in range(CK):
                        xk = [a[:, k, t * P:(t + 1) * P] for a in (x_hi, x_lo)]
                        w = [a[:, k, c0:c0 + NKV * HD] for a in (wq_hi, wq_lo)]
                        ins = three_pass(ps[:, t * C:(t + 1) * C], xk, w, k, k == CK - 1)
                ins.then_inc(filled, 1)

            def near(b, j):
                ps = claim("near", b, j)
                wait_for(pe, "rotated", b, j + 1)
                mm(ps[:, :], k_T[:, j // 4, 0:P], q_T[:, j % 4].rearrange("p h q -> p (h q)"),
                   start=True, stop=True).then_inc(filled, 1)

            def far(b, i):
                ps = claim("far", b, i)
                wait_for(pe, "rotated", b, 2 * i + 2)
                s = (2 * i) % 4
                mm(ps[:].rearrange("p (h q) -> p h q", h=4), k_T[:, i // 2, P:T],
                   q_T[:, s:s + 2, :, P:T].rearrange("p a h q -> p (a h) q"),
                   start=True, stop=True).then_inc(filled, 1)

            def mix(b, i):
                j, t = divmod(i, 2)
                ps = claim("mix", b, i)
                pe.wait_ge(consts_set, CONSTS)
                wait_for(pe, "values", b)
                wait_for(pe, "causal", b, tile_at["near", j])
                if t:
                    wait_for(pe, "causal", b, tile_at["far", j // 2])
                for m in range(2):
                    o = ps[:, m * (HD + 1):(m + 1) * (HD + 1)]
                    ins = mm(o, p_near[:, j % NEAR, m, t * P:(t + 1) * P], v_s[:, 0, j // 4, :],
                             start=True, stop=(t == 0))
                    if t:
                        ins = mm(o, p_far[:, (j // 2) % 2, 2 * (j % 2) + m, :], v_s[:, 1, j // 4, :],
                                 start=False, stop=True)
                ins.then_inc(filled, 1)

            def turn(b, j):
                ps = claim("turn", b, j)
                if b == 0:
                    pe.wait_ge(tables_in, 48)
                wait_for(pe, "attn", b, 2 * j + 1)
                for m in range(2):
                    for t in range(TT):
                        ins = transpose(ps[:, m * T + t * P:m * T + (t + 1) * P], a_s[:, j % 2, t, m, :], ident_s[:])
                ins.then_inc(filled, 1)

            def proj(b, j):
                wait_for(pe, "attn_T", b, j)
                if j == 0:
                    for t in range(TT):
                        wait_for(pe, "ln1", b - 1, 0, t)
                    if b == 0:
                        pe.wait_ge(wo_in, 16)
                for t in range(TT):
                    for m in range(2):
                        ins = mm(acc[:, t, :], a_T[:, j % 2, m, t * P:(t + 1) * P], wo_s[:, 2 * j + m, :],
                                 start=(j == 0 and t == 0 and m == 0), stop=(j == PAIRS - 1 and m == 1),
                                 skip_group_check=True)
                ins.then_inc(sig["projected", 0], 1)

            def turn_w(i):
                ps = claim("turn_w", 0, i, 0, 0)[:].bitcast(BF16)
                pe.wait_ge(consts_set, CONSTS)
                pe.wait_ge(quant_w, 7 * (i + 1))
                for k in range(CK):
                    for o in range(CK):
                        ins = transpose(ps[:, k * C + o * P:k * C + (o + 1) * P], q_int[:, o, k * P:(k + 1) * P],
                                        identb_s[:])
                ins.then_inc(filled, 1)
                ps = claim("turn_w", 0, i, 0, 1)
                pe.wait_ge(scale_diag, CK * (i + 1))
                for o in range(CK):
                    ins = mm(ps[:, o * P:(o + 1) * P], ones[:], q_tmp[:, o, 0:P], start=True, stop=True)
                ins.then_inc(filled, 1)

            def context(b, t):
                ps = claim("ctx", b, t)
                pe.wait_ge(ctx_in, 16 * (b + 1))
                pe.wait_ge(wkv_in, 16)
                for k in range(CK):
                    ins = mm(ps[:, :], ctx_s[:, k, t * P:(t + 1) * P], wkv_s[:, k, :], start=(k == 0), stop=(k == CK - 1))
                ins.then_inc(filled, 1)

            def turn_ints(kind, b, t, signal):
                ps = claim(kind, b, 0, t)[:].bitcast(BF16)
                wait_for(pe, signal, b, 5, t)
                for k in range(CK):
                    ins = transpose(ps[:, k * P:(k + 1) * P], q_int[:, t, k * P:(k + 1) * P], identb_s[:])
                ins.then_inc(filled, 1)

            def int_product(kind, b, t, signal, w):
                ps = claim(kind, b, 0, t)
                wait_for(pe, signal, b, 0, t)
                if b == 0:
                    pe.wait_ge(xw_T_done, w + 1)
                for k in range(CK):
                    ins = mm(ps[:, 0:C], q_intT[:, t, k, :], xw_T[:, w, k, :], start=(k == 0), stop=(k == CK - 1))
                ins.then_inc(filled, 1)

            def stacked(t, h):
                return parts[:, t, h:h + 2].rearrange("p h l c -> p (h l c)").bitcast(F32)

            def turn_k(b, g):
                ps = claim("turn_k", b, g)
                pe.wait_ge(tables_in, 48)
                wait_for(pe, "kv", b, 7)
                for m2 in range(2):
                    for k in range(TT):
                        ins = transpose(ps[:, m2 * T + k * P:m2 * T + (k + 1) * P], stacked(k, 4 * g + 2 * m2), ident_s[:])
                ins.then_inc(filled, 1)

            def turn_q(b, g, t):
                ps = claim("turn_q", b, g, t)
                wait_for(pe, "query", b, 3, t)
                for m2 in range(2):
                    ins = transpose(ps[:, m2 * P:(m2 + 1) * P], stacked(t, 4 * g + 2 * m2), ident_s[:])
                ins.then_inc(filled, 1)

            def xscore(b, g, t):
                ps = [claim("xscore", b, g, t, m) for m in range(2)]
                wait_for(pe, "k_T", b, g)
                wait_for(pe, "q_T", b, g, t)
                for m in range(2):
                    r = slice(64 * m, 64 * m + 64)
                    for m2 in range(2):
                        ins = mm(ps[m][:, m2 * T:(m2 + 1) * T], qS[r, t, g % 2, m2, :], kS[r, g, m2, :],
                                 start=True, stop=True)
                    ins.then_inc(filled, 1)

            def turn_p(b, i, t):
                ps = claim("turn_p", b, i, t)
                g, m = divmod(i, 2)
                for m2 in range(2):
                    wait_for(pe, "xexp", b, 2 * i + m2, t)
                    for k in range(TT):
                        ins = transpose(ps[:, m2 * T + k * P:m2 * T + (k + 1) * P], xs[:, t, m, m2, k * P:(k + 1) * P],
                                        ident_s[:])
                ins.then_inc(filled, 1)

            def xmix(b, g, t):
                ps = claim("xmix", b, g, t)
                wait_for(pe, "probs_T_even", b, g, t)
                wait_for(pe, "probs_T_odd", b, g, t)
                wait_for(pe, "kv", b, 5)
                for k in range(TT):
                    for h in range(4):
                        ins = mm(ps[XW * h:XW * (h + 1), 0:P], xv_s[:, k, 4 * g + h, :], xp_T[:, t, h % 2, h // 2, k, :],
                                 start=(k == 0), stop=(k == TT - 1))
                ins.then_inc(filled, 1)

            def turn_o(b, t):
                ps = claim("turn_o", b, 0, t)
                wait_for(pe, "xout", b, QUADS - 1, t)
                for g in range(QUADS):
                    ins = transpose(ps[:, g * P:(g + 1) * P], xo_T[:, t, g, :], ident_s[:])
                ins.then_inc(filled, 1)

            def turn_z(b, t):
                ps = claim("turn_z", b, 0, t)
                wait_for(pe, "ln2", b, 5, t)
                for k in range(CK):
                    ins = transpose(ps[:, k * P:(k + 1) * P], z[b % 2][:, t, k * P:(k + 1) * P], ident_s[:])
                ins.then_inc(filled, 1)

            def route(b, t):
                ps = claim("route", b, 0, t)
                wait_for(pe, "z_T", b, 0, t)
                if b == 0:
                    pe.wait_ge(route_in, 32)
                for k in range(CK):
                    ins = mm(ps[0:NBLK, 0:P], wr_s[:, k, :], z_T[:, t, k, :], start=(k == 0), stop=(k == CK - 1))
                ins.then_inc(filled, 1)

            def turn_r(b, t):
                ps = claim("turn_r", b, 0, t)
                wait_for(pe, "logits", b, 0, t)
                transpose(ps[:, 0:NBLK], lg_T[:, t * P:(t + 1) * P], ident_s[0:NBLK, 0:NBLK]).then_inc(filled, 1)

            def turn_m(b, t):
                ps = claim("turn_m", b, 0, t)[:].bitcast(BF16)
                wait_for(pe, "route", b, 10, t)
                transpose(ps[0:NBLK, 0:P], keep[:, t, :], identb_s[:]).then_inc(filled, 1)

            def hidden(b, part, t):
                if b == 0:
                    pe.wait_ge(ffn_in, 32)
                n = HT // HPARTS
                ps = claim("hidden", b, part, t, 0)
                for m in range(n):
                    for k in range(CK):
                        ins = mm(ps[:, m * P:(m + 1) * P], w1_s[:, k, (n * part + m) * P:(n * part + m + 1) * P],
                                 z_T[:, t, k, :], start=(k == 0), stop=(k == CK - 1))
                ins.then_inc(filled, 1)
                ps = claim("hidden", b, part, t, 1)
                wait_for(pe, "mask_T", b, 0, t)
                for m in range(n):
                    ins = mm(ps[:, m * P:(m + 1) * P], pick_s[:, n * part + m, :], keep_T[:, t * P:(t + 1) * P],
                             start=True, stop=True)
                ins.then_inc(filled, 1)

            def ffn(b, t):
                ps = claim("ffn", b, 0, t)
                for n in range(HT):
                    if n % (HT // HPARTS) == 0:
                        wait_for(pe, "masked", b, n * HPARTS // HT, t)
                    ins = mm(ps[:, 0:C], g_T[:, t, n, :], w2_s[:, n, :], start=(n == 0), stop=(n == HT - 1))
                ins.then_inc(filled, 1)

            for kind, b, i, t in plan:
                if kind == "rot":
                    rot(b, i)
                elif kind == "val":
                    val(b)
                elif kind == "near":
                    near(b, i)
                elif kind == "far":
                    far(b, i)
                elif kind == "mix":
                    mix(b, i)
                elif kind == "turn":
                    turn(b, i)
                elif kind == "proj":
                    proj(b, i)
                elif kind == "turn_w":
                    turn_w(i)
                elif kind == "ctx":
                    context(b, i)
                elif kind == "turn_x":
                    turn_ints(kind, b, t, "quant_y")
                elif kind == "query":
                    int_product(kind, b, t, "y_T", 0)
                elif kind == "turn_k":
                    turn_k(b, i)
                elif kind == "turn_q":
                    turn_q(b, i, t)
                elif kind == "xscore":
                    xscore(b, i, t)
                elif kind == "turn_p":
                    turn_p(b, i, t)
                elif kind == "xmix":
                    xmix(b, i, t)
                elif kind == "turn_o":
                    turn_o(b, t)
                elif kind == "turn_ox":
                    turn_ints(kind, b, t, "quant_o")
                elif kind == "outproj":
                    int_product(kind, b, t, "o_T", 1)
                elif kind == "turn_z":
                    turn_z(b, t)
                elif kind == "route":
                    route(b, t)
                elif kind == "turn_r":
                    turn_r(b, t)
                elif kind == "turn_m":
                    turn_m(b, t)
                elif kind == "hidden":
                    hidden(b, i, t)
                elif kind == "ffn":
                    ffn(b, t)

        @block.scalar
        def _(act):
            activation, copy = nc.scalar.activation, nc.scalar.copy

            def evacuate(dst, src, kind, b, i, t, name):
                wait_filled(act, kind, b, i, t)
                copy(dst, src).then_inc(sig[name, t], 1)

            def split_piece(n):
                act.wait_ge(piece_in[n], 16)
                c = PIECES - 1 if n == 0 else n - 1
                for h in range(2):
                    copy(wq_hi[:, :, c * PW + h * PAIR:c * PW + (h + 1) * PAIR], stage[:, n % 3, :, h * PAIR:(h + 1) * PAIR])\
                        .then_inc(piece_hi, 1)

            def split_x(b):
                act.wait_ge(x_in, 16 * (b + 1))
                wait_filled(act, "rot", b - 1, PAIRS)
                copy(x_hi[:], xT_s[:]).then_inc(sig["x_hi", 0], 1)

            def val(b):
                wait_filled(act, "val", b)
                wait_filled(act, "mix", b - 1, NH - 1)
                copy(v_s[:, :, :, 0:HD], bank("val", b)[:].rearrange("p (t g d) -> p t g d", t=TT, g=NKV))\
                    .then_inc(sig["values", 0], 1)
                if b + 1 < B:
                    wait_for(act, "x_lo", b)
                    act.dma_start(xT_s[:], xT[b + 1].rearrange("(k p) n -> p k n", p=P)).then_inc(x_in, 16)

            def score(kind, b, i):
                n = tile_at[kind, i]
                if kind == "near":
                    dst = p_near[:, i % NEAR].rearrange("p h q -> p (h q)")
                    prev = (b, 2 * (i - NEAR) + 1) if i >= NEAR else (b - 1, 2 * range(i, PAIRS, NEAR)[-1] + 1)
                else:
                    dst = p_far[:, i % 2].rearrange("p h q -> p (h q)")
                    prev = (b, 4 * (i - 2) + 3) if i >= 2 else (b - 1, 4 * (i + QUADS - 2) + 3)
                wait_filled(act, "mix", *prev)
                wait_filled(act, kind, b, i)
                activation(dst, bank(kind, b, i)[:], ACT.Tanh, scale=SCALE / SOFTCAP).then_inc(sig["capped", 0], 1)
                wait_for(act, "capped", b, n)
                activation(dst, dst, ACT.Exp, scale=SOFTCAP).then_inc(sig["expd", 0], 1)

            def turn(b, j):
                if j < 2:
                    wait_for(act, "projected", b - 1, PAIRS - 2 + j)
                else:
                    wait_for(act, "projected", b, j - 2)
                evacuate(a_T[:, j % 2].rearrange("p h q -> p (h q)"), bank("turn", b, j)[:], "turn", b, j, 0, "attn_T")

            def turn_w(i):
                wait_filled(act, "turn_w", 0, i, 0, 0)
                copy(xw_T[:, i].rearrange("p k c -> p (k c)"), bank("turn_w", 0, i, 0, 0)[:].bitcast(BF16)[:, 0:CK * C])\
                    .then_inc(xw_T_done, 1)

            def turn_k(b, g):
                for t in range(TT):
                    wait_filled(act, "xscore", b - 1, g, t, 1)
                evacuate(kS[:, g].rearrange("p a k -> p (a k)"), bank("turn_k", b, g)[:], "turn_k", b, g, 0, "k_T")

            def turn_q(b, g, t):
                wait_filled(act, "xscore", *((b, g - 2) if g >= 2 else (b - 1, g + QUADS - 2)), t, 1)
                evacuate(qS[:, t, g % 2].rearrange("p a q -> p (a q)"), bank("turn_q", b, g, t)[:, 0:2 * P],
                         "turn_q", b, g, t, "q_T")

            def xexp(b, g, t):
                for m in range(2):
                    for m2 in range(2):
                        wait_for(act, "xmasked", b, 4 * g + 2 * m + m2, t)
                        activation(xs[:, t, m, m2, :], xs[:, t, m, m2, :], ACT.Exp, bias=xneg[:, t, m, m2:m2 + 1], scale=-1.0)\
                            .then_inc(sig["xexp", t], 1)

            def turn_p(b, i, t):
                g, m = divmod(i, 2)
                if m == 0:
                    wait_filled(act, "xmix", *((b, g - 1) if g else (b - 1, QUADS - 1)), t)
                    evacuate(xp_T[:, t, 0].rearrange("p m k q -> p (m k q)"), bank("turn_p", b, i, t)[:],
                             "turn_p", b, i, t, "probs_T_even")

            def route_exp(b, t):
                wait_for(act, "route", b, 1, t)
                activation(prob[:, t, :], r_in[:, t, :], ACT.Exp).then_inc(sig["route_exp", t], 1)

            def hidden(b, part, t):
                wait_filled(act, "ffn", b - 1, 0, t)
                n = HT // HPARTS
                wait_filled(act, "hidden", b, part, t, 0)
                activation(g_T[:, t, n * part:n * (part + 1), :].rearrange("p h n -> p (h n)"),
                           bank("hidden", b, part, t, 0)[:], ACT.Gelu).then_inc(sig["gelu", t], 1)

            for kind, b, i, t in plan:
                if kind == "split_x":
                    split_x(b)
                elif kind == "piece":
                    split_piece(i)
                elif kind == "val":
                    val(b)
                elif kind in ("near", "far"):
                    score(kind, b, i)
                elif kind == "turn":
                    turn(b, i)
                elif kind == "turn_w":
                    turn_w(i)
                elif kind == "turn_k":
                    turn_k(b, i)
                elif kind == "turn_q":
                    turn_q(b, i, t)
                elif kind == "xscore":
                    xexp(b, i, t)
                elif kind == "turn_p":
                    turn_p(b, i, t)
                elif kind == "turn_x":
                    evacuate(q_intT[:, t].rearrange("p k q -> p (k q)"), bank(kind, b, 0, t)[:].bitcast(BF16)[:, 0:CK * P],
                             kind, b, 0, t, "y_T")
                elif kind == "turn_ox":
                    evacuate(q_intT[:, t].rearrange("p k q -> p (k q)"), bank(kind, b, 0, t)[:].bitcast(BF16)[:, 0:CK * P],
                             kind, b, 0, t, "o_T")
                elif kind == "xmix":
                    wait_filled(act, "turn_o", b - 1, 0, t)
                    evacuate(xo_T[:, t, i, :], bank(kind, b, i, t)[:, 0:P], kind, b, i, t, "xout")
                elif kind == "turn_z":
                    wait_filled(act, "hidden", b - 1, HPARTS - 1, t, 0)
                    evacuate(z_T[:, t].rearrange("p k q -> p (k q)"), bank(kind, b, 0, t)[:, 0:CK * P], kind, b, 0, t, "z_T")
                elif kind == "route":
                    wait_filled(act, "turn_r", b - 1, 0, t)
                    wait_filled(act, kind, b, 0, t)
                    activation(lg_T[:, t * P:(t + 1) * P], bank(kind, b, 0, t)[0:NBLK, 0:P], ACT.Identity, bias=br_s[:])\
                        .then_inc(sig["logits", t], 1)
                elif kind == "turn_r":
                    route_exp(b, t)
                elif kind == "turn_m":
                    wait_filled(act, "hidden", b - 1, HPARTS - 1, t, 1)
                    evacuate(keep_T[:, t * P:(t + 1) * P], bank(kind, b, 0, t)[0:NBLK, :].bitcast(BF16)[:, 0:P],
                             kind, b, 0, t, "mask_T")
                elif kind == "hidden":
                    hidden(b, i, t)

        @block.vector
        def _(dve):
            v = nc.vector

            def steps(semaphore, base):
                n = [base]

                def do(ins):
                    ins.then_inc(semaphore, 1)
                    n[0] += 1

                def done():
                    dve.wait_ge(semaphore, n[0])
                return do, done

            def split_piece(n):
                c = PIECES - 1 if n == 0 else n - 1
                for h in range(2):
                    dve.wait_ge(piece_hi, 2 * n + h + 1)
                    cols = slice(c * PW + h * PAIR, c * PW + (h + 1) * PAIR)
                    v.tensor_tensor(wq_lo[:, :, cols], stage[:, n % 3, :, h * PAIR:(h + 1) * PAIR],
                                    wq_hi[:, :, cols].bitcast(F32), ALU.subtract).then_inc(piece_lo, 1)

            def split_x(b):
                wait_for(dve, "x_hi", b)
                v.tensor_tensor(x_lo[:], xT_s[:], x_hi[:].bitcast(F32), ALU.subtract).then_inc(sig["x_lo", 0], 1)

            def rope(b, i):
                ps = bank("rot", b, i)[:].rearrange("p (h q) -> p h q", h=2)
                n = b * (PAIRS + 1) + i
                if n >= 2:
                    dve.wait_ge(sig["rotated", 0], n - 1)
                if i == 0:
                    wait_filled(dve, "far", b - 1, QUADS - 1)
                    dst = k_T[:]
                else:
                    j = i - 1
                    wait_filled(dve, "far", *((b, (j - 4) // 2) if j >= 4 else (b - 1, (j + PAIRS - 4) // 2)))
                    dst = q_T[:, j % 4]
                wait_filled(dve, "rot", b, i)
                if b == 0:
                    dve.wait_ge(tables_in, 48)
                c, s = (a[:].unsqueeze(1).to_broadcast([P, 2, T]) for a in (cos_s, sin_s))
                v.tensor_tensor(dst, ps, c, ALU.mult).then_inc(sig["roped", 0], 1)
                lower, upper = slice(0, HD // 2), slice(HD // 2, HD)
                t = rope_t[:, n % 2]
                v.tensor_tensor(t[lower], ps[upper], s[upper], ALU.mult).then_inc(sig["roped", 0], 1)
                v.tensor_tensor(t[upper], ps[lower], s[lower], ALU.mult).then_inc(sig["roped", 0], 1)

            def mix(b, i):
                j, t = divmod(i, 2)
                wait_filled(dve, "mix", b, i)
                if j < 2:
                    wait_filled(dve, "turn", b - 1, PAIRS - 2 + j)
                else:
                    wait_filled(dve, "turn", b, j - 2)
                ps = bank("mix", b, i)[:, 0:2 * (HD + 1)].rearrange("p (h d) -> p h d", h=2)
                rec = a_rec[:, i % 2, :].unsqueeze(2)
                v.reciprocal(rec, ps[:, :, HD:HD + 1]).then_inc(sig["attn_rec", 0], 1)
                wait_for(dve, "attn_rec", b, i)
                v.tensor_tensor(a_s[:, j % 2, t], ps[:, :, 0:HD], rec.to_broadcast([P, 2, HD]), ALU.mult)\
                    .then_inc(sig["attn", 0], 1)

            def layer_norm(n, b, t, do, done, h, y):
                done()
                do(v.bn_stats(stats[n][:, t, :], h[:, t, :]))
                done()
                do(v.bn_aggr(moments[n][:, t, :], stats[n][:, t, :]))
                done()
                do(v.tensor_scalar(var_eps[n][:, t:t + 1], moments[n][:, t, 1:2], EPS_LN, None, ALU.add))
                wait_for(dve, f"rstd{n + 1}", b, 0, t)
                do(v.tensor_scalar(y[:, t, :], h[:, t, :], moments[n][:, t, 0:1], rstd[n][:, t:t + 1],
                                   ALU.subtract, ALU.mult))

            def norm1(b, t):
                wait_for(dve, "projected", b, PAIRS - 1)
                dve.wait_ge(xtok_in[b % 2], 16 * (b // 2 + 1))
                do, done = steps(sig["ln1", t], b * PER_TILE["ln1"])
                h = y1[:, b % 2]
                do(v.tensor_tensor(h[:, t, :], acc[:, t, :], h[:, t, :], ALU.add))
                layer_norm(0, b, t, do, done, h, h)

            def quantise(src, do, done, tiles):
                c = slice(tiles[0], tiles[-1] + 1)
                do(v.tensor_reduce(q_amax[:, c], src[:, c], AX_X, ALU.max, apply_absolute_value=True))
                done()
                do(v.tensor_scalar(q_scale[:, c], q_amax[:, c], 1.0 / QMAX, EPS_Q, ALU.mult, ALU.max))
                done()
                do(v.reciprocal(q_rs[:, c], q_scale[:, c]))
                done()
                for a in tiles:
                    do(v.tensor_scalar(q_tmp[:, a, :], src[:, a, :], q_rs[:, a:a + 1], QMAX, ALU.mult, ALU.min))
                done()
                do(v.tensor_scalar(q_tmp[:, c], q_tmp[:, c], -QMAX, ROUND, ALU.max, ALU.add))
                done()
                do(v.tensor_scalar(q_int[:, c], q_tmp[:, c], ROUND, None, ALU.subtract))

            def quant_weight(i):
                src = (z[0], y1[:, 1])[i]
                dve.wait_ge(xw_in, 32)
                do, done = steps(quant_w, 7 * i)
                if i:
                    wait_filled(dve, "turn_w", 0, 0, 0, 1)
                quantise(src, do, done, range(TT))
                done()
                for o in range(CK):
                    v.tensor_scalar(q_tmp[:, o, 0:P], ident_s[:], q_scale[:, o:o + 1], None, ALU.mult)\
                        .then_inc(scale_diag, 1)

            def turn_w(i):
                factor = XD ** -0.5 if i == 0 else 1.0
                wait_filled(dve, "turn_w", 0, i, 0, 1)
                v.tensor_scalar(xw_scale[:, i, :], bank("turn_w", 0, i, 0, 1)[:, 0:C], factor, None, ALU.mult)\
                    .then_inc(xw_scale_done, 1)
                if i == 0:
                    dve.wait_ge(xbias_in, 16)
                    v.tensor_scalar(bias_s[:, 0, :], bias_s[:, 0, :], factor, None, ALU.mult).then_inc(bias_scaled, 1)

            def context(b, t):
                do, done = steps(sig["kv", 0], b * PER["kv"] + 4 * t)
                wait_filled(dve, "ctx", b, t)
                wait_filled(dve, "turn_q", b - 1, QUADS - 1, t)
                if t == 0:
                    for a in range(TT):
                        wait_filled(dve, "xmix", b - 1, QUADS - 1, a)
                    if b == 0:
                        dve.wait_ge(xbias_in, 16)
                ps = bank("ctx", b, t)
                both = lambda a: a.rearrange("p (h c) -> p h c", h=XH).unsqueeze(2).to_broadcast([P, XH, 2, XD])
                hi, lo = parts[:, t, :, 0:4:2, :], parts[:, t, :, 1:4:2, :]
                do(v.tensor_tensor(lo.bitcast(F32), both(ps[:, 0:C]), both(bias_s[:, 1, :]), ALU.add))
                do(v.tensor_tensor(xv_s[:, t, :, 0:XD], ps[:, C:2 * C].rearrange("p (h c) -> p h c", h=XH),
                                   bias_s[:, 2, :].rearrange("p (h c) -> p h c", h=XH), ALU.add))
                done()
                do(v.tensor_copy(hi, lo.bitcast(F32)))
                done()
                do(v.tensor_tensor(lo, lo.bitcast(F32), hi.bitcast(F32), ALU.subtract))

            def quant_x(b, t):
                wait_filled(dve, "turn_ox", b - 1, 0, t)
                if b == 0:
                    wait_filled(dve, "turn_w", 0, 1, 0, 0)
                do, done = steps(sig["quant_y", t], b * PER_TILE["quant_y"])
                wait_for(dve, "ln1", b, 4, t)
                wait_for(dve, "ln2", b - 1, 5, t)
                quantise(y1[:, b % 2], do, done, [t])

            def dequantise(ps, w, t, do):
                do(v.scalar_tensor_tensor(q_tmp[:, t, :], ps[:, 0:C], q_scale[:, t:t + 1], xw_scale[:, w, :],
                                          ALU.mult, ALU.mult))

            def query(b, t):
                wait_filled(dve, "query", b, 0, t)
                if b == 0:
                    dve.wait_ge(xw_scale_done, 2)
                    dve.wait_ge(bias_scaled, 1)
                do, done = steps(sig["query", t], b * PER_TILE["query"])
                dequantise(bank("query", b, 0, t), 0, t, do)
                done()
                do(v.tensor_tensor(q_tmp[:, t, :], q_tmp[:, t, :], bias_s[:, 0, :], ALU.add))
                done()
                wait_filled(dve, "turn_k", b, QUADS - 1)
                q = q_tmp[:, t, :].rearrange("p (h c) -> p h c", h=XH).unsqueeze(2).to_broadcast([P, XH, 2, XD])
                do(v.tensor_copy(parts[:, t, :, 0:2, :], q))
                done()
                do(v.tensor_tensor(parts[:, t, :, 2:4, :], q, parts[:, t, :, 0:2, :].bitcast(F32), ALU.subtract))

            def xscore(b, g, t):
                do, _ = steps(sig["xmasked", t], b * PER_TILE["xmasked"] + 4 * g)
                if g == 0:
                    wait_for(dve, "mask_neg", b, 0, t)
                for m in range(2):
                    wait_filled(dve, "turn_p", *((b, 2 * (g - 1) + m) if g else (b - 1, 2 * (QUADS - 1) + m)), t)
                    wait_filled(dve, "xscore", b, g, t, m)
                    for m2 in range(2):
                        do(v.tensor_tensor_reduce(out=xs[:, t, m, m2, :], in0=bank("xscore", b, g, t, m)[:, m2 * T:(m2 + 1) * T],
                                                  in1=mask_s[:, t, :], scale=-1.0, scalar=3.0e38, op0=ALU.add,
                                                  op1=ALU.min, accum_out=xneg[:, t, m, m2:m2 + 1]))

            def turn_p(b, i, t):
                g, m = divmod(i, 2)
                if m:
                    wait_filled(dve, "xmix", *((b, g - 1) if g else (b - 1, QUADS - 1)), t)
                    wait_filled(dve, "turn_p", b, i, t)
                    v.tensor_copy(xp_T[:, t, 1].rearrange("p m k q -> p (m k q)"), bank("turn_p", b, i, t)[:])\
                        .then_inc(sig["probs_T_odd", t], 1)

            def turn_o(b, t):
                wait_filled(dve, "turn_o", b, 0, t)
                wait_for(dve, "query", b, 3, t)
                ps = bank("turn_o", b, 0, t)[:].rearrange("p (h w) -> p h w", w=XW)
                rec = xrec[:, t, :].unsqueeze(2)
                v.reciprocal(rec, ps[:, :, XD:XD + 1]).then_inc(sig["xattn", t], 1)
                wait_for(dve, "xattn", b, 0, t)
                v.tensor_tensor(q_tmp[:, t, :].rearrange("p (h c) -> p h c", h=XH), ps[:, :, 0:XD],
                                rec.to_broadcast([P, XH, XD]), ALU.mult).then_inc(sig["xattn", t], 1)

            def quant_o(b, t):
                do, done = steps(sig["quant_o", t], b * PER_TILE["quant_o"])
                wait_for(dve, "xattn", b, 1, t)
                quantise(q_tmp, do, done, [t])

            def outproj(b, t):
                wait_filled(dve, "outproj", b, 0, t)
                do, done = steps(sig["ln2", t], b * PER_TILE["ln2"])
                dequantise(bank("outproj", b, 0, t), 1, t, do)
                done()
                wait_for(dve, "y1_bias", b, 0, t)
                do(v.tensor_tensor(q_tmp[:, t, :], q_tmp[:, t, :], y1[:, b % 2, t, :], ALU.add))
                wait_filled(dve, "turn_z", b - 2, 0, t)
                wait_for(dve, "ln3", b - 2, 0, t)
                layer_norm(1, b, t, do, done, q_tmp, z[b % 2])

            def router(b, t):
                do, done = steps(sig["route", t], b * PER_TILE["route"])
                wait_filled(dve, "turn_r", b, 0, t)
                ps = bank("turn_r", b, 0, t)[:, 0:NBLK]
                do(v.tensor_reduce(r_max[:, t:t + 1], ps, AX_X, ALU.max))
                done()
                do(v.tensor_scalar(r_in[:, t, :], ps, r_max[:, t:t + 1], None, ALU.subtract))
                wait_for(dve, "route_exp", b, 0, t)
                do(v.tensor_reduce(r_sum[:, t:t + 1], prob[:, t, :], AX_X, ALU.add))
                done()
                do(v.reciprocal(r_rec[:, t:t + 1], r_sum[:, t:t + 1]))
                done()
                do(v.tensor_scalar(prob[:, t, :], prob[:, t, :], r_rec[:, t:t + 1], None, ALU.mult))
                done()
                other = prob[:, t, :].unsqueeze(1).to_broadcast([P, NBLK, NBLK])
                own = prob[:, t, :].unsqueeze(2).to_broadcast([P, NBLK, NBLK])
                do(v.tensor_tensor(above[:, t], other, own, ALU.is_gt))
                do(v.tensor_tensor(equal[:, t], other, own, ALU.is_equal))
                done()
                if b == 0:
                    dve.wait_ge(consts_set, CONSTS)
                do(v.tensor_tensor(equal[:, t], equal[:, t], before_s[:], ALU.mult))
                done()
                do(v.tensor_tensor(above[:, t], above[:, t], equal[:, t], ALU.add))
                done()
                do(v.tensor_reduce(rank[:, t, :], above[:, t], AX_X, ALU.add))
                done()
                wait_filled(dve, "turn_m", b - 1, 0, t)
                do(v.tensor_scalar(keep[:, t, :], rank[:, t, :], TOPK - 0.5, None, ALU.is_lt))

            def hidden(b, part, t):
                n = HT // HPARTS
                g = g_T[:, t, n * part:n * (part + 1), :].rearrange("p h n -> p (h n)")
                wait_for(dve, "gelu", b, part, t)
                wait_filled(dve, "hidden", b, part, t, 1)
                v.tensor_tensor(g, g, bank("hidden", b, part, t, 1)[:], ALU.mult).then_inc(sig["masked", t], 1)

            def ffn(b, t):
                wait_filled(dve, "ffn", b, 0, t)
                do, done = steps(sig["ln3", t], b * PER_TILE["ln3"])
                if b:
                    dve.wait_ge(sig["stored", t], 16 * b)
                do(v.tensor_tensor(y3[:, t, :], bank("ffn", b, 0, t)[:, 0:C], z[b % 2][:, t, :], ALU.add))
                layer_norm(2, b, t, do, done, y3, y3)

            for kind, b, i, t in plan:
                if kind == "split_x":
                    split_x(b)
                elif kind == "piece":
                    split_piece(i)
                elif kind == "rot":
                    rope(b, i)
                elif kind == "mix":
                    mix(b, i)
                elif kind == "norm1":
                    norm1(b, t)
                elif kind == "quant_w":
                    quant_weight(i)
                elif kind == "turn_w":
                    turn_w(i)
                elif kind == "ctx":
                    context(b, i)
                elif kind == "quant_x":
                    quant_x(b, t)
                elif kind == "query":
                    query(b, t)
                elif kind == "xscore":
                    xscore(b, i, t)
                elif kind == "turn_p":
                    turn_p(b, i, t)
                elif kind == "turn_o":
                    turn_o(b, t)
                elif kind == "quant_o":
                    quant_o(b, t)
                elif kind == "outproj":
                    outproj(b, t)
                elif kind == "turn_r":
                    router(b, t)
                elif kind == "hidden":
                    hidden(b, i, t)
                elif kind == "ffn":
                    ffn(b, t)

        @block.gpsimd
        def _(pool):
            g = nc.gpsimd

            def constants():
                def select(out, pattern, base, channel, op):
                    g.affine_select(out=out, in_=out, compare_op=op, fill=0.0, base=base, pattern=pattern,
                                    channel_multiplier=channel).then_inc(consts_set, 1)

                g.memset(ones[:], 1.0).then_inc(consts_set, 1)
                g.memset(half[:], -0.5).then_inc(consts_set, 1)
                g.memset(v_s[:, :, :, HD:HD + 1], 1.0).then_inc(consts_set, 1)
                g.memset(xv_s[:, :, :, XD:XD + 1], 1.0).then_inc(consts_set, 1)
                g.memset(xv_s[:, :, :, XD + 1:XW], 0.0).then_inc(consts_set, 1)
                g.memset(identb_s[:], 1.0).then_inc(consts_set, 1)
                g.memset(pick_s[:], 1.0).then_inc(consts_set, 1)
                g.memset(before_s[:], 1.0).then_inc(consts_set, 1)
                pool.wait_ge(consts_set, 8)
                select(identb_s[:], [[-1, P]], 0, 1, ALU.is_equal)
                select(before_s[:], [[1, NBLK], [-1, NBLK]], 0, 0, ALU.is_gt)
                select(pick_s[:], [[P, HT], [1, P]], 0, -BLK, ALU.is_ge)
                pool.wait_ge(consts_set, 11)
                select(pick_s[:], [[-P, HT], [-1, P]], BLK - 1, BLK, ALU.is_ge)

            def rotate(b, i):
                n = b * (PAIRS + 1) + i
                dst = k_T[:] if i == 0 else q_T[:, (i - 1) % 4]
                wait_for(pool, "roped", b, 3 * i + 2)
                g.tensor_tensor(dst, dst, rope_t[:, n % 2], ALU.add).then_inc(sig["rotated", 0], 1)

            def causal(kind, b, i):
                wait_for(pool, "expd", b, tile_at[kind, i])
                p, heads = (p_near[:, i % NEAR, :, 0:P], 2) if kind == "near" else (p_far[:, i % 2], 4)
                g.affine_select(out=p, in_=p, compare_op=ALU.is_ge, fill=0.0, base=0,
                                pattern=[[0, heads], [1, P]], channel_multiplier=-1).then_inc(sig["causal", 0], 1)

            def add_bias(b, t):
                wait_for(pool, "quant_y", b, 3, t)
                g.tensor_tensor(y1[:, b % 2, t, :], y1[:, b % 2, t, :], bias_s[:, 3, :], ALU.add).then_inc(sig["y1_bias", t], 1)

            def negate_mask(b, t):
                pool.wait_ge(mask_in, 16 * (b + 1))
                g.tensor_scalar(mask_s[:, t, :], mask_s[:, t, :], -1.0, None, ALU.mult).then_inc(sig["mask_neg", t], 1)

            def inverse_root(n, b, name, step, t):
                wait_for(pool, name, b, step, t)
                c = slice(t, t + 1)
                g.tensor_tensor(rstd[n][:, c], var_eps[n][:, c], half[:, c], ALU.pow).then_inc(sig[f"rstd{n + 1}", t], 1)

            constants()
            pool.wait_ge(consts_set, CONSTS)
            for kind, b, i, t in plan:
                if kind == "rot":
                    rotate(b, i)
                elif kind in ("near", "far"):
                    causal(kind, b, i)
                elif kind == "norm1":
                    inverse_root(0, b, "ln1", 3, t)
                elif kind == "quant_x":
                    negate_mask(b, t)
                    add_bias(b, t)
                elif kind == "outproj":
                    inverse_root(1, b, "ln2", 4, t)
                elif kind == "ffn":
                    inverse_root(2, b, "ln3", 3, t)


def rope_tables():
    freq = (np.float32(1.0) / np.float32(10000.0) ** (np.arange(0, HD, 2, dtype=np.float32) / np.float32(HD)))
    angle = np.outer(freq.astype(np.float32), np.arange(T, dtype=np.float32)).astype(np.float32)
    cos, sin = np.cos(angle), np.sin(angle)
    return np.concatenate([cos, cos]), np.concatenate([sin, -sin])


def kernel(**inputs):
    import concourse.bacc as bacc
    from concourse.bass_utils import run_bass_kernel_spmd

    a = {k: np.asarray(v) for k, v in inputs.items()}
    cos, sin = rope_tables()
    arrays = {
        "x": a["x"],
        "xT": a["x"].transpose(0, 2, 1),
        "ctxT": a["ctx_2048"].transpose(0, 2, 1),
        "mask": a["mask_BxSxS2_ff0"],
        "wqkv": a["L0_attn_Wqkv"],
        "wo": a["L0_attn_Wo"],
        "wkvT": np.concatenate([a["L0_xattn_wk"].T, a["L0_xattn_wv"].T], 1),
        "xwq": a["L0_xattn_wq"],
        "xwo": a["L0_xattn_wo"],
        "xbias": np.concatenate([a[f"L0_xattn_b{n}"] for n in "qkvo"]),
        "wrT": a["L0_ffn_Wr"].T,
        "br": a["L0_ffn_br"].reshape(NBLK, 1),
        "w1T": a["L0_ffn_W1"].T,
        "w2T": a["L0_ffn_W2"].T,
        "cos": cos,
        "sin": sin,
        "ident": np.eye(P, dtype=np.float32),
    }
    arrays = {f"in_{k}": np.ascontiguousarray(v) for k, v in arrays.items()}
    nc = bacc.Bacc("TRN2", target_bir_lowering=False, num_devices=1)
    args = [nc.dram_tensor(k, v.shape, mybir.dt.from_np(v.dtype), kind="ExternalInput").ap() for k, v in arrays.items()]
    out = nc.dram_tensor("out_y", (B, T, C), F32, kind="ExternalOutput").ap()
    build_decoder(nc, *args, out)
    r = run_bass_kernel_spmd(nc, [arrays], core_ids=[0])
    return r.results[0]["out_y"]
```
